# Optimizing a Trainium2 kernel written in Bass

```python
import numpy as np
import jax
import jax.numpy as jnp

def _softmax(x, axis=-1):
    return jax.nn.softmax(x, axis=axis)

def _gelu(x):
    return jax.nn.gelu(x, approximate=True)

def _silu(x):
    return jax.nn.silu(x)

def _sigmoid(x):
    return jax.nn.sigmoid(x)

def _layernorm(x, axis=-1, eps=1e-05):
    m = jnp.mean(x, axis=axis, keepdims=True)
    v = jnp.var(x, axis=axis, keepdims=True)
    return (x - m) / jnp.sqrt(v + eps)

def _scatter_add(tgt, idx, src, axis=0):
    return tgt.at[idx].add(src)

def _segment_sum(src, seg, n):
    return jax.ops.segment_sum(src, seg, n)
kernel_name = 'mk_sandwich_d1_jaxref_r4_25b501'

def setup_inputs(seed: int=0):
    np.random.seed(seed)
    _w = jnp.asarray

    def _L0_attn_setup():
        import jax, jax.numpy as jnp
        import numpy as np
        B, S, H, HS, BLK = (4, 1024, 16, 256, 64)
        D = HS // H
        key = jax.random.key(seed)
        ks = jax.random.split(key, 7)
        s = np.float32(1.0 / np.sqrt(HS))
        return {'hidden_states': jax.random.normal(ks[0], (B, S, HS), jnp.float32), 'Wq': jax.random.normal(ks[1], (HS, HS), jnp.float32) * s, 'bq': jax.random.normal(ks[2], (HS,), jnp.float32) * s, 'Wk': jax.random.normal(ks[3], (HS, HS), jnp.float32) * s, 'bk': jax.random.normal(ks[4], (HS,), jnp.float32) * s, 'Wv': jax.random.normal(ks[5], (HS, HS), jnp.float32) * s, 'bv': jax.random.normal(ks[6], (HS,), jnp.float32) * s}
    _L0_attn_in = _L0_attn_setup()

    def _L0_ffn_setup():
        import jax, jax.numpy as jnp
        import numpy as np
        from jax.scipy.linalg import expm
        B, S, D, E, K, NROT = (2, 512, 256, 8, 2, 3)
        EPS = 1e-05

        def _gelu(x):
            return jax.nn.gelu(x, approximate=False)

        def _forward(x, ln_gamma, ln_beta, abel_w, abel_b, moe_gate_w, moe_gate_b, ew1, eb1, ew2, eb2, gens, gc_w, gc_b):
            residual = x
            mu = jnp.mean(x, axis=-1, keepdims=True)
            var = jnp.mean((x - mu) ** 2, axis=-1, keepdims=True)
            xn = (x - mu) * jax.lax.rsqrt(var + EPS) * ln_gamma + ln_beta
            abel_out = _gelu(xn @ abel_w + abel_b)
            logits = xn @ moe_gate_w + moe_gate_b
            topw, topi = jax.lax.top_k(logits, K)
            topw = jax.nn.softmax(topw, axis=-1)
            w_dense = jnp.sum(jax.nn.one_hot(topi, E, dtype=xn.dtype) * topw[..., None], axis=-2)
            h = _gelu(jnp.einsum('bsd,edh->ebsh', xn, ew1) + eb1[:, None, None, :])
            eo = jnp.einsum('ebsh,ehd->ebsd', h, ew2) + eb2[:, None, None, :]
            moe_out = jnp.einsum('ebsd,bse->bsd', eo, w_dense)
            for i in range(NROT):
                moe_out = moe_out @ expm(gens[i])
            combined = jnp.concatenate([abel_out, moe_out], axis=-1)
            gate = jax.nn.sigmoid(combined @ gc_w + gc_b)
            mixed = abel_out * (1.0 - gate) + moe_out * gate
            return residual + mixed
        key = jax.random.key(seed)
        ks = jax.random.split(key, 16)
        sc = 0.02
        x = jax.random.normal(ks[0], (B, S, D), jnp.float32)
        ln_gamma = 1.0 + sc * jax.random.normal(ks[1], (D,), jnp.float32)
        ln_beta = sc * jax.random.normal(ks[2], (D,), jnp.float32)
        abel_w = sc * jax.random.normal(ks[3], (D, D), jnp.float32)
        abel_b = sc * jax.random.normal(ks[4], (D,), jnp.float32)
        moe_gate_w = sc * jax.random.normal(ks[5], (D, E), jnp.float32)
        moe_gate_b = sc * jax.random.normal(ks[6], (E,), jnp.float32)
        ew1 = sc * jax.random.normal(ks[7], (E, D, 2 * D), jnp.float32)
        eb1 = sc * jax.random.normal(ks[8], (E, 2 * D), jnp.float32)
        ew2 = sc * jax.random.normal(ks[9], (E, 2 * D, D), jnp.float32)
        eb2 = sc * jax.random.normal(ks[10], (E, D), jnp.float32)
        g = sc * jax.random.normal(ks[11], (NROT, D, D), jnp.float32)
        gens = 0.5 * (g - jnp.swapaxes(g, -1, -2))
        gc_w = sc * jax.random.normal(ks[12], (2 * D, 1), jnp.float32)
        gc_b = sc * jax.random.normal(ks[13], (1,), jnp.float32)
        return dict(x=x, ln_gamma=ln_gamma, ln_beta=ln_beta, abel_w=abel_w, abel_b=abel_b, moe_gate_w=moe_gate_w, moe_gate_b=moe_gate_b, ew1=ew1, eb1=eb1, ew2=ew2, eb2=eb2, gens=gens, gc_w=gc_w, gc_b=gc_b)
    _L0_ffn_in = _L0_ffn_setup()
    _d = {'L0_attn_hidden_states': _L0_attn_in['hidden_states'], 'L0_attn_Wq': _L0_attn_in['Wq'], 'L0_attn_bq': _L0_attn_in['bq'], 'L0_attn_Wk': _L0_attn_in['Wk'], 'L0_attn_bk': _L0_attn_in['bk'], 'L0_attn_Wv': _L0_attn_in['Wv'], 'L0_attn_bv': _L0_attn_in['bv'], 'L0_ffn_ln_gamma': _L0_ffn_in['ln_gamma'], 'L0_ffn_ln_beta': _L0_ffn_in['ln_beta'], 'L0_ffn_abel_w': _L0_ffn_in['abel_w'], 'L0_ffn_abel_b': _L0_ffn_in['abel_b'], 'L0_ffn_moe_gate_w': _L0_ffn_in['moe_gate_w'], 'L0_ffn_moe_gate_b': _L0_ffn_in['moe_gate_b'], 'L0_ffn_ew1': _L0_ffn_in['ew1'], 'L0_ffn_eb1': _L0_ffn_in['eb1'], 'L0_ffn_ew2': _L0_ffn_in['ew2'], 'L0_ffn_eb2': _L0_ffn_in['eb2'], 'L0_ffn_gens': _L0_ffn_in['gens'], 'L0_ffn_gc_w': _L0_ffn_in['gc_w'], 'L0_ffn_gc_b': _L0_ffn_in['gc_b']}
    _x0 = _d['L0_attn_hidden_states']
    _d['L0_attn_hidden_states'] = jax.random.normal(jax.random.fold_in(jax.random.key(seed), 1), (16, 512, 256), dtype=_x0.dtype)
    del _x0
    return _d

def reference(L0_attn_hidden_states, L0_attn_Wq, L0_attn_bq, L0_attn_Wk, L0_attn_bk, L0_attn_Wv, L0_attn_bv, L0_ffn_ln_gamma, L0_ffn_ln_beta, L0_ffn_abel_w, L0_ffn_abel_b, L0_ffn_moe_gate_w, L0_ffn_moe_gate_b, L0_ffn_ew1, L0_ffn_eb1, L0_ffn_ew2, L0_ffn_eb2, L0_ffn_gens, L0_ffn_gc_w, L0_ffn_gc_b):

    def _L0_attn_ref(hidden_states, Wq, bq, Wk, bk, Wv, bv):
        import jax, jax.numpy as jnp
        import numpy as np
        B, S, H, HS, BLK = (4, 1024, 16, 256, 64)
        D = HS // H
        b, m, _ = hidden_states.shape
        h, d, wm = (H, D, BLK)
        wn = wm
        nb = m // wm
        scale = np.float32(1.0 / np.sqrt(d))

        def heads(x):
            return x.reshape(b, m, h, d).transpose(0, 2, 1, 3)
        q = heads(hidden_states @ Wq.T + bq)
        k = heads(hidden_states @ Wk.T + bk)
        v = heads(hidden_states @ Wv.T + bv)
        qb = q.reshape(b, h, nb, wm, d)
        kb = k.reshape(b, h, nb, wn, d)
        vb = v.reshape(b, h, nb, wn, d)

        def attend(qx, kx, vx):
            scores = jnp.einsum('bhqd,bhkd->bhqk', qx, kx) * scale
            return jnp.einsum('bhqk,bhkd->bhqd', jax.nn.softmax(scores, axis=-1), vx)
        first_ctx = attend(qb[:, :, 0], k, v)[:, :, None]
        k2 = jnp.concatenate([kb[:, :, 0], kb[:, :, 1], kb[:, :, 2], kb[:, :, -1]], axis=2)
        v2 = jnp.concatenate([vb[:, :, 0], vb[:, :, 1], vb[:, :, 2], vb[:, :, -1]], axis=2)
        second_ctx = attend(qb[:, :, 1], k2, v2)[:, :, None]
        exp_k = jnp.concatenate([kb[:, :, 1:-3], kb[:, :, 2:-2], kb[:, :, 3:-1]], axis=3)
        exp_v = jnp.concatenate([vb[:, :, 1:-3], vb[:, :, 2:-2], vb[:, :, 3:-1]], axis=3)
        mq = qb[:, :, 2:-2]
        inner = jnp.einsum('bhlqd,bhlkd->bhlqk', mq, exp_k) * scale
        first_band = jnp.einsum('bhlqd,bhkd->bhlqk', mq, kb[:, :, 0]) * scale
        last_band = jnp.einsum('bhlqd,bhkd->bhlqk', mq, kb[:, :, -1]) * scale
        band = jnp.concatenate([first_band, inner, last_band], axis=-1)
        aw = jax.nn.softmax(band, axis=-1)
        mid_ctx = jnp.einsum('bhlqk,bhlkd->bhlqd', aw[..., wn:4 * wn], exp_v)
        mid_ctx = mid_ctx + jnp.einsum('bhlqk,bhkd->bhlqd', aw[..., :wn], vb[:, :, 0])
        mid_ctx = mid_ctx + jnp.einsum('bhlqk,bhkd->bhlqd', aw[..., -wn:], vb[:, :, -1])
        k3 = jnp.concatenate([kb[:, :, 0], kb[:, :, -3], kb[:, :, -2], kb[:, :, -1]], axis=2)
        v3 = jnp.concatenate([vb[:, :, 0], vb[:, :, -3], vb[:, :, -2], vb[:, :, -1]], axis=2)
        second_last_ctx = attend(qb[:, :, -2], k3, v3)[:, :, None]
        last_ctx = attend(qb[:, :, -1], k, v)[:, :, None]
        ctx = jnp.concatenate([first_ctx, second_ctx, mid_ctx, second_last_ctx, last_ctx], axis=2)
        return ctx.reshape(b, h, m, d).transpose(0, 2, 1, 3).reshape(b, m, h * d)

    def _L0_ffn_ref(x, ln_gamma, ln_beta, abel_w, abel_b, moe_gate_w, moe_gate_b, ew1, eb1, ew2, eb2, gens, gc_w, gc_b):
        import jax, jax.numpy as jnp
        import numpy as np
        from jax.scipy.linalg import expm
        B, S, D, E, K, NROT = (2, 512, 256, 8, 2, 3)
        EPS = 1e-05

        def _gelu(x):
            return jax.nn.gelu(x, approximate=False)

        def _forward(x, ln_gamma, ln_beta, abel_w, abel_b, moe_gate_w, moe_gate_b, ew1, eb1, ew2, eb2, gens, gc_w, gc_b):
            residual = x
            mu = jnp.mean(x, axis=-1, keepdims=True)
            var = jnp.mean((x - mu) ** 2, axis=-1, keepdims=True)
            xn = (x - mu) * jax.lax.rsqrt(var + EPS) * ln_gamma + ln_beta
            abel_out = _gelu(xn @ abel_w + abel_b)
            logits = xn @ moe_gate_w + moe_gate_b
            topw, topi = jax.lax.top_k(logits, K)
            topw = jax.nn.softmax(topw, axis=-1)
            w_dense = jnp.sum(jax.nn.one_hot(topi, E, dtype=xn.dtype) * topw[..., None], axis=-2)
            h = _gelu(jnp.einsum('bsd,edh->ebsh', xn, ew1) + eb1[:, None, None, :])
            eo = jnp.einsum('ebsh,ehd->ebsd', h, ew2) + eb2[:, None, None, :]
            moe_out = jnp.einsum('ebsd,bse->bsd', eo, w_dense)
            for i in range(NROT):
                moe_out = moe_out @ expm(gens[i])
            combined = jnp.concatenate([abel_out, moe_out], axis=-1)
            gate = jax.nn.sigmoid(combined @ gc_w + gc_b)
            mixed = abel_out * (1.0 - gate) + moe_out * gate
            return residual + mixed
        return _forward(x, ln_gamma, ln_beta, abel_w, abel_b, moe_gate_w, moe_gate_b, ew1, eb1, ew2, eb2, gens, gc_w, gc_b)
    x = L0_attn_hidden_states
    x = x + _layernorm(_L0_attn_ref(_layernorm(x, axis=-1), L0_attn_Wq, L0_attn_bq, L0_attn_Wk, L0_attn_bk, L0_attn_Wv, L0_attn_bv), axis=-1)
    x = x + _layernorm(_L0_ffn_ref(_layernorm(x, axis=-1), L0_ffn_ln_gamma, L0_ffn_ln_beta, L0_ffn_abel_w, L0_ffn_abel_b, L0_ffn_moe_gate_w, L0_ffn_moe_gate_b, L0_ffn_ew1, L0_ffn_eb1, L0_ffn_ew2, L0_ffn_eb2, L0_ffn_gens, L0_ffn_gc_w, L0_ffn_gc_b), axis=-1)
    return x

_drawn_inputs = setup_inputs


def setup_inputs(seed=0):
    import zlib

    import numpy as np

    out = dict(_drawn_inputs(seed))
    spreads = {}
    factors = {'L0_attn_bk': 64.0,
     'L0_ffn_ln_gamma': 8.0,
     'L0_ffn_ln_beta': 8.0,
     'L0_ffn_abel_b': 8.0,
     'L0_ffn_moe_gate_w': 5.445,
     'L0_ffn_moe_gate_b': 8.0,
     'L0_ffn_ew1': 4.991,
     'L0_ffn_eb1': 21.676,
     'L0_ffn_ew2': 4.865,
     'L0_ffn_eb2': 64.0,
     'L0_ffn_gens': 8.0,
     'L0_ffn_gc_w': 8.0}
    for name, (base, spread) in spreads.items():
        noise = np.random.default_rng([zlib.crc32(name.encode()), seed]).standard_normal(out[name].shape)
        drawn = base * np.exp(spread * noise) if base else spread * noise
        out[name] = jnp.asarray(drawn.astype(out[name].dtype))
    for name, factor in factors.items():
        out[name] = (out[name] * factor).astype(out[name].dtype)
    return out
```

```python
from contextlib import ExitStack

import concourse.bass as bass
from concourse import mybir

F32 = mybir.dt.float32
BF16 = mybir.dt.bfloat16
I32 = mybir.dt.int32
U32 = mybir.dt.uint32
ALU = mybir.AluOpType
ACT = mybir.ActivationFunctionType
AX_X = mybir.AxisListType.X

P = 128
EPS = 1e-5
HEADS, DH, BLK = 16, 16, 64

ORDER = [1, 2, 0, 7, 3, 4, 5, 6]
MEETS = [[(0, 320)], [(0, 512)], [(64, 448)], [(128, 256), (320, 512)]]
NT = len(MEETS)
CHUNKS = [
    [(1, 0, 0, 512)],
    [(0, 0, 0, 320), (2, 320, 64, 256)],
    [(2, 0, 256, 448), (3, 192, 128, 256), (3, 320, 320, 512)],
]
NCH = len(CHUNKS)
RUNS = [(0, 1, 2), (2, 0, 1), (3, 7, 1), (4, 3, 2), (6, 5, 2)]

Q_PART = [0, 0, 1, 1, 0, 2]
K_PART = [0, 1, 0, 1, 2, 0]
NGRP = len(Q_PART)
MASK_ROW = NGRP * DH
N_MASK = 4
MAX_ROW = MASK_ROW + N_MASK
N_MAX = 2
K_SCORE = MAX_ROW
K_EXP = MAX_ROW + N_MAX
BIG = 1e30
HOLES = [((1, 5), (3,)), ((2, 6), (4,)), ((3,), (1, 5)), ((4,), (2, 6))]

GROUP = 4
NG = HEADS // GROUP
UNITS = HEADS * NCH
QUADS = UNITS // GROUP
NPB = 8
B_FROM = 4


def tile(ap, t):
    return ap[:, t * P:(t + 1) * P]


def attention(nc, outer, x, xs, wqkvT, bqk, bv_rep, ident, qrows, krows):
    B, S, D = x.shape
    NTOK = S // P
    KC = D // P
    assert D == HEADS * DH and S == 8 * BLK
    ctx = ExitStack()
    with ctx:
        def sb(name, shape, dt=F32):
            return ctx.enter_context(nc.sbuf_tensor(name, shape, dt))

        def ps(name, shape, dt=F32):
            return ctx.enter_context(nc.psum_tensor(name, shape, dt))

        def sem(name):
            return outer.enter_context(nc.semaphore(name))

        wqkv = sb("wqkv", [P, KC, 3 * D])
        bqk_sb = sb("bqk_sb", [P, 4])
        bv_sb = sb("bv_sb", [P, 2, D])
        ident_sb = sb("ident_sb", [P, P])
        neg_half = sb("neg_half", [P, NTOK])
        stat = sb("stat", [P, NTOK, 6])
        mv = sb("mv", [P, NTOK, 2])
        veps = sb("veps", [P, NTOK])
        rstd = sb("rstd", [P, NTOK])
        xn = sb("xn", [P, NTOK, D])
        xnT = sb("xnT", [P, KC, S])
        split = sb("split", [P, 4, 3, S], BF16)
        resid = sb("resid", [P, 2, S])
        rows_sb = resid
        qst = [sb(f"qst{i}", [P, HEADS, S], BF16) for i in range(2)]
        kst = [sb(f"kst{i}", [P, HEADS, S], BF16) for i in range(2)]
        vaug = [sb(f"vaug{i}", [P, NT, HEADS, 32]) for i in range(2)]
        mx = sb("mx", [P, NT * HEADS])
        mrow = sb("mrow", [NT * HEADS, N_MAX, P], BF16)
        pexp = sb("pexp", [P, NPB, S])
        ctxT = sb("ctxT", [P, NG, S])
        rden = sb("rden", [P, 2, HEADS])
        ctxn = sb("ctxn", [P, NTOK, D])
        cstat = sb("cstat", [P, NTOK, 6])
        cmv = sb("cmv", [P, NTOK, 2])
        cveps = sb("cveps", [P, NTOK])
        crstd = sb("crstd", [P, NTOK])

        work = [ps(f"work{i}", [P, S]) for i in range(4)]
        scT = [ps(f"scT{i}", [P, S]) for i in range(2)]
        pv = ps("pv", [P, S])
        turn = ps("turn", [P, S])

        spill = nc.dram_tensor("split_spill", [2, 4, P, 3, S], BF16, kind="Internal").ap()

        s_const = sem("s_const")
        s_rows = sem("s_rows")
        s_xin = [sem(f"s_xin{i}") for i in range(2)]
        s_stat = sem("s_stat")
        s_veps = sem("s_veps")
        s_rstd = sem("s_rstd")
        s_xn = sem("s_xn")
        s_bn = sem("s_bn")
        w_full = [sem(f"w_full{i}") for i in range(4)]
        w_free = [sem(f"w_free{i}") for i in range(4)]
        s_part1 = sem("s_part1")
        s_res = sem("s_res")
        s_part2 = sem("s_part2")
        s_split = sem("s_split")
        s_spill = [sem(f"s_spill{i}") for i in range(2)]
        s_stack = [sem(f"s_stack{i}") for i in range(2)]
        s_m1 = sem("s_m1")
        s_mrow = sem("s_mrow")
        s_sc = sem("s_sc")
        s_exp = sem("s_exp")
        s_pv = sem("s_pv")
        s_ctxT = sem("s_ctxT")
        s_turn = sem("s_turn")
        s_rden = sem("s_rden")
        s_ctxn = sem("s_ctxn")
        s_cbn = sem("s_cbn")
        s_cstat = sem("s_cstat")
        s_cveps = sem("s_cveps")
        s_crstd = sem("s_crstd")
        s_cln = sem("s_cln")
        s_x1 = sem("s_x1")
        s_vpad = sem("s_vpad")
        N_CONST = 6

        W_USES = [19, 18, 18, 18]
        block = ctx.enter_context(nc.Block())

        def wait(eng, s, value):
            if not isinstance(value, int) or value > 0:
                eng.wait_ge(s, value)

        def plain(eng):
            eng.nop(nofuse=True)

        def steps(eng, step):
            for s in range(2):
                step(s, s % 2)
            with eng.Fori(1, B // 2 - 1) as i:
                step(2 * i, 0)
                step(2 * i + 1, 1)
            for s in range(B - 2, B + 2):
                step(s, s % 2)

        def nth_load(b, par):
            return (b + 2 - par) // 2

        def doing(s):
            if not isinstance(s, int):
                return True, True, True
            return s < B, 1 <= s <= B, 2 <= s

        def load_x(sp, b, par):
            for pos, blk, n in RUNS:
                lo = pos % 2 * BLK
                sp.dma_start(xs[lo:lo + n * BLK, b, pos // 2, :], x[b, blk * BLK:(blk + n) * BLK, :])\
                  .then_inc(s_xin[par], 16)

        @block.sync
        def _(sp):
            sp.dma_start(ident_sb[:, :], ident).then_inc(s_const, 16)
            sp.dma_start(wqkv[:, :, :], wqkvT.rearrange("(k p) o -> p k o", p=P)).then_inc(s_const, 16)
            sp.dma_start(bqk_sb[:, :], bqk).then_inc(s_const, 16)
            sp.dma_start(bv_sb[:, :, :], bv_rep).then_inc(s_const, 16)
            sp.dma_start(rows_sb[MASK_ROW:K_EXP, 0, :], qrows).then_inc(s_const, 16)
            sp.dma_start(rows_sb[MASK_ROW:K_EXP, 1, :], krows).then_inc(s_const, 16)
            load_x(sp, 0, 0)
            load_x(sp, 1, 1)

            def step(s, par):
                project, attend, finish = doing(s)
                if not project:
                    return
                b = s
                if not isinstance(b, int) or b + 2 < B:
                    sp.wait_ge(s_bn, (b + 1) * NTOK)
                    load_x(sp, b + 2, par)
                wait(sp, s_sc, (b - 1) * UNITS)
                plain(sp)
                if isinstance(b, int) and b < 2:
                    sp.wait_ge(s_rows, 4)
                for half in range(2):
                    for m in range(2 * half, 2 * half + 2):
                        sp.wait_ge(s_split, b * 4 + m + 1)
                        sp.dma_start(spill[par, m], split[:, m, :, :]).then_inc(s_spill[half], 16)
                    sp.wait_ge(s_spill[half], b * 32 + 32)
                    for st, m, parts in ((qst, 2 * half, Q_PART), (kst, 2 * half + 1, K_PART)):
                        for g, part in enumerate(parts):
                            src = spill[par, m].rearrange("(h d) s c -> d h s c", d=DH)[:, :, part, :]
                            sp.dma_start(st[par][g * DH:(g + 1) * DH, 8 * half:8 * half + 8, :], src)\
                              .then_inc(s_stack[half], 16)
                sp.wait_ge(w_free[0], b * W_USES[0] + W_USES[0])
                for t in range(NT):
                    for part in range(N_MAX):
                        r = MAX_ROW + part
                        sp.dma_start(qst[par][r:r + 1, :, t * P:(t + 1) * P],
                                     mrow[t * HEADS:(t + 1) * HEADS, part, :]).then_inc(s_mrow, 16)

            steps(sp, step)

        @block.tensor
        def _(pe):
            pe.wait_ge(s_const, N_CONST * 16)

            def use(w, b, n):
                wait(pe, w_free[w], b * W_USES[w] + n)

            def turn_xn(b):
                for k in range(KC):
                    use(k, b, 0)
                    for j in range(NTOK):
                        pe.wait_ge(s_xn, b * NTOK + j + 1)
                        ins = nc.tensor.transpose(work[k][:, j * P:(j + 1) * P],
                                                  xn[:, j, k * P:(k + 1) * P], ident_sb[:, :])
                    ins.then_inc(w_full[k], 1)

            def project(b, par):
                for m in range(4):
                    w = (2 + m) % 4
                    col = (m % 2) * D + (m // 2) * P
                    if m == 0:
                        for k in range(KC):
                            pe.wait_ge(w_free[k], b * W_USES[k] + 1)
                    use(w, b, 0 if m < 2 else 1)
                    for k in range(KC):
                        ins = nc.tensor.matmul(work[w][:, :], wqkv[:, k, col:col + P], xnT[:, k, :],
                                               start=(k == 0), stop=(k == KC - 1))
                    ins.then_inc(w_full[w], 1)
                for w in (2, 3):
                    use(w, b, 1)
                    for n in range(2):
                        for k in range(KC):
                            ins = nc.tensor.matmul(work[w][:, n * D:(n + 1) * D],
                                                   tile(xnT[:, k, :], 2 * (w - 2) + n),
                                                   wqkv[:, k, 2 * D:3 * D], start=(k == 0), stop=(k == KC - 1))
                    ins.then_inc(w_full[w], 1)

            def max_unit(b, par, h, t):
                if t == 0 and h % 8 == 0:
                    pe.wait_ge(s_stack[h // 8], (b + 1) * 2 * NGRP * 16)
                use(t, b, 2 + h)
                at = 0
                for lo, hi in MEETS[t]:
                    ins = nc.tensor.matmul(work[t][:, at:at + hi - lo], tile(qst[par][0:K_SCORE, h, :], t),
                                           kst[par][0:K_SCORE, h, lo:hi], start=True, stop=True)
                    at += hi - lo
                ins.then_inc(w_full[t], 1)

            def turn_max(b):
                for t in range(NT):
                    pe.wait_ge(w_free[t], b * W_USES[t] + 2 + HEADS)
                plain(pe)
                nc.tensor.transpose(work[0][0:NT * HEADS, 0:P], mx[:, :], ident_sb[:, :]).then_inc(w_full[0], 1)

            def score_unit(b, par, q, n):
                h, c = q // NCH * GROUP + n, q % NCH
                u = b * UNITS + q * GROUP + n
                if q == 0 and n == 0:
                    pe.wait_ge(s_mrow, (b + 1) * NT * N_MAX * 16)
                wait(pe, s_exp, u - 1)
                for t, at, lo, hi in CHUNKS[c]:
                    ins = nc.tensor.matmul(scT[n % 2][:, at:at + hi - lo],
                                           tile(kst[par][0:K_EXP, h, :], t),
                                           qst[par][0:K_EXP, h, lo:hi], start=True, stop=True)
                ins.then_inc(s_sc, 1)

            def pv_quad(b, par, q):
                g, c = q // NCH, q % NCH
                pe.wait_ge(s_exp, b * UNITS + (q + 1) * GROUP)
                if q == 0:
                    for w in (2, 3):
                        pe.wait_ge(w_free[w], b * W_USES[w] + 2)
                if c == 0:
                    wait(pe, s_ctxT, b * NG + g)
                for t, at, lo, hi in CHUNKS[c]:
                    for n in range(GROUP):
                        h = g * GROUP + n
                        last = c == NCH - 1 and (t, at, lo, hi) == CHUNKS[c][-1]
                        ins = nc.tensor.matmul(pv[32 * n:32 * n + 32, lo:hi], vaug[par][:, t, h, :],
                                               pexp[:, (q * GROUP + n) % NPB, at:at + hi - lo],
                                               start=(c == 0), stop=last, skip_group_check=True)
                ins.then_inc(s_pv, 1)

            def turn_ctx(b, j):
                if j == 0:
                    pe.wait_ge(s_ctxT, (b + 1) * NG)
                wait(pe, s_ctxn, b * NTOK + j)
                for g in range(NG):
                    ins = nc.tensor.transpose(turn[:, g * P:(g + 1) * P], ctxT[:, g, j * P:(j + 1) * P],
                                              ident_sb[:, :])
                ins.then_inc(s_turn, 1)

            def step(s, par):
                proj, attend, finish = doing(s)
                if proj:
                    turn_xn(s)
                    project(s, par)
                units = [(h, t) for h in range(HEADS) for t in range(NT)] if proj else []
                for q in range(QUADS):
                    if finish and q < NTOK:
                        turn_ctx(s - 2, q)
                    fill = units[(q - B_FROM) * 8:(q - B_FROM + 1) * 8] if q >= B_FROM else []
                    if attend:
                        for n in range(GROUP):
                            score_unit(s - 1, 1 - par, q, n)
                            if n > 0:
                                for h, t in fill[(n - 1) * 3:n * 3]:
                                    max_unit(s, par, h, t)
                        if q > 0:
                            pv_quad(s - 1, 1 - par, q - 1)
                    else:
                        for h, t in fill:
                            max_unit(s, par, h, t)
                if proj:
                    turn_max(s)
                if attend:
                    pv_quad(s - 1, 1 - par, QUADS - 1)

            steps(pe, step)

        @block.scalar
        def _(act):
            act.wait_ge(s_const, N_CONST * 16)

            def evac_xnT(b):
                for k in range(KC):
                    act.wait_ge(w_full[k], b * W_USES[k] + 1)
                    nc.scalar.copy(xnT[:, k, :], work[k][:, :]).then_inc(w_free[k], 1)

            def first_part(b):
                for m in range(4):
                    w = (2 + m) % 4
                    act.wait_ge(w_full[w], b * W_USES[w] + (1 if m < 2 else 2))
                    if m % 2 == 0:
                        wait(act, s_spill[m // 2], b * 32)
                    nc.scalar.activation(split[:, m, 0, :], work[w][:, :], ACT.Identity,
                                         bias=bqk_sb[:, m:m + 1]).then_inc(s_part1, 1)

            def first_max(b):
                act.wait_ge(w_full[0], b * W_USES[0] + W_USES[0])
                wait(act, s_mrow, b * NT * N_MAX * 16)
                nc.scalar.copy(mrow[:, 0, :], work[0][0:NT * HEADS, 0:P]).then_inc(s_m1, 1)

            def exps(b, q):
                for n in range(GROUP):
                    u = b * UNITS + q * GROUP + n
                    act.wait_ge(s_sc, u + 1)
                    if n == 0:
                        wait(act, s_pv, b * QUADS + q - NPB // GROUP + 1)
                    nc.scalar.activation(pexp[:, (q * GROUP + n) % NPB, :], scT[n % 2][:, :], ACT.Exp,
                                         scale=DH ** -0.5).then_inc(s_exp, 1)

            def evac_ctx(b, g):
                act.wait_ge(s_pv, b * QUADS + (g + 1) * NCH)
                if g == 0:
                    wait(act, s_turn, b * NTOK)
                nc.scalar.copy(ctxT[:, g, :], pv[:, :]).then_inc(s_ctxT, 1)

            def step(s, par):
                proj, attend, finish = doing(s)
                if proj:
                    evac_xnT(s)
                    first_part(s)
                if attend:
                    for q in range(QUADS):
                        exps(s - 1, q)
                        if q > 0 and q % NCH == 0:
                            evac_ctx(s - 1, q // NCH - 1)
                if proj:
                    first_max(s)
                if attend:
                    evac_ctx(s - 1, NG - 1)

            steps(act, step)

        @block.vector
        def _(dve):
            nc.vector.memset(neg_half[:, :], -0.5).then_inc(s_rows, 1)
            for i in range(2):
                nc.vector.memset(vaug[i][:, :, :, DH:32], 0.0).then_inc(s_vpad, 1)
            dve.wait_ge(s_vpad, 2)
            for i in range(2):
                nc.vector.memset(vaug[i][:, :, :, DH:DH + 1], 1.0).then_inc(s_vpad, 1)
            dve.wait_ge(s_const, N_CONST * 16)
            for i in range(2):
                for st, r in ((qst, 0), (kst, 1)):
                    src = rows_sb[MASK_ROW:K_EXP, r, :].rearrange("p (o c) -> p o c", o=1)
                    nc.vector.tensor_copy(st[i][MASK_ROW:K_EXP, :, :],
                                          src.broadcast_to([K_EXP - MASK_ROW, HEADS, S])).then_inc(s_rows, 1)

            def stats(b):
                for j in range(NTOK):
                    nc.vector.bn_stats(stat[:, j, :], xs[:, b, j, :]).then_inc(s_bn, 1)
                dve.wait_ge(s_bn, (b + 1) * NTOK)
                plain(dve)
                for j in range(NTOK):
                    nc.vector.bn_aggr(mv[:, j, :], stat[:, j, :]).then_inc(s_stat, 1)

            def normalise(b):
                dve.wait_ge(s_rstd, b + 1)
                for j in range(NTOK):
                    nc.vector.tensor_scalar(xn[:, j, :], xs[:, b, j, :], mv[:, j, 0:1], rstd[:, j:j + 1],
                                            ALU.subtract, ALU.mult).then_inc(s_xn, 1)

            def parts(b):
                for m in range(4):
                    w = (2 + m) % 4
                    dve.wait_ge(s_part1, b * 4 + m + 1)
                    nc.vector.scalar_tensor_tensor(out=resid[:, m % 2, :], in0=work[w][:, :],
                                                   scalar=bqk_sb[:, m:m + 1], in1=split[:, m, 0, :],
                                                   op0=ALU.add, op1=ALU.subtract).then_inc(w_free[w], 1)
                    dve.wait_ge(w_free[w], b * W_USES[w] + (1 if m < 2 else 2))
                    nc.vector.tensor_copy(split[:, m, 1, :], resid[:, m % 2, :]).then_inc(s_part2, 1)
                    dve.wait_ge(s_part2, b * 4 + m + 1)
                    nc.vector.tensor_tensor(split[:, m, 2, :], resid[:, m % 2, :], split[:, m, 1, :],
                                            ALU.subtract).then_inc(s_split, 1)

            def values(b, par):
                for n in range(2):
                    dve.wait_ge(w_full[2 + n], b * W_USES[2 + n] + 2)
                    nc.vector.tensor_tensor(
                        vaug[par][:, 2 * n:2 * n + 2, :, 0:DH],
                        work[2 + n][:, :].rearrange("p (t h d) -> p t h d", t=2, d=DH),
                        bv_sb[:, :, :].rearrange("p t (h d) -> p t h d", d=DH), ALU.add)\
                      .then_inc(w_free[2 + n], 1)

            def maximum(b, h, t):
                dve.wait_ge(w_full[t], b * W_USES[t] + 3 + h)
                n = sum(hi - lo for lo, hi in MEETS[t])
                c = t * HEADS + h
                nc.vector.reduce_max(mx[:, c:c + 1], work[t][:, 0:n], AX_X).then_inc(w_free[t], 1)

            def second_max(b):
                dve.wait_ge(s_m1, b + 1)
                nc.vector.tensor_tensor(mrow[:, 1, :], work[0][0:NT * HEADS, 0:P], mrow[:, 0, :],
                                        ALU.subtract).then_inc(w_free[0], 1)

            def finish_a(b, j):
                dve.wait_ge(s_turn, b * NTOK + j + 1)
                tv = turn[:, :].rearrange("p (h e) -> p h e", e=32)
                nc.vector.reciprocal(rden[:, j % 2, :], tv[:, :, DH]).then_inc(s_rden, 1)
                dve.wait_ge(s_rden, b * NTOK + j + 1)
                if j == 0:
                    wait(dve, s_x1, b * NTOK)
                inv = rden[:, j % 2, :].rearrange("p (h o) -> p h o", o=1).broadcast_to([P, HEADS, DH])
                nc.vector.tensor_tensor(ctxn[:, j, :].rearrange("p (h d) -> p h d", d=DH),
                                        tv[:, :, 0:DH], inv, ALU.mult).then_inc(s_ctxn, 1)
                dve.wait_ge(s_ctxn, b * NTOK + j + 1)
                nc.vector.bn_stats(cstat[:, j, :], ctxn[:, j, :]).then_inc(s_cbn, 1)
                dve.wait_ge(s_cbn, b * NTOK + j + 1)
                plain(dve)
                nc.vector.bn_aggr(cmv[:, j, :], cstat[:, j, :]).then_inc(s_cstat, 1)

            def finish_b(b):
                dve.wait_ge(s_crstd, b + 1)
                for j in range(NTOK):
                    nc.vector.tensor_scalar(ctxn[:, j, :], ctxn[:, j, :], cmv[:, j, 0:1], crstd[:, j:j + 1],
                                            ALU.subtract, ALU.mult).then_inc(s_cln, 1)

            def step(s, par):
                proj, attend, finish = doing(s)
                if isinstance(s, int) and s == 0:
                    dve.wait_ge(s_xin[0], len(RUNS) * 16)
                    stats(0)
                    normalise(0)
                if proj:
                    parts(s)
                    values(s, par)
                if finish:
                    for j in range(NTOK):
                        finish_a(s - 2, j)
                more = not isinstance(s, int) or s + 1 < B
                if more:
                    dve.wait_ge(s_xin[1 - par], nth_load(s + 1, 1 - par) * len(RUNS) * 16)
                    stats(s + 1)
                if finish:
                    finish_b(s - 2)
                units = [(h, t) for h in range(HEADS) for t in range(NT)] if proj else []
                if more:
                    normalise(s + 1)
                for h, t in units:
                    maximum(s, h, t)
                if proj:
                    second_max(s)

            steps(dve, step)

        @block.gpsimd
        def _(pool):
            pool.wait_ge(s_rows, 1)

            def inverse(n, ready, per, var, mid, mid_sem, dst, dst_sem):
                pool.wait_ge(ready, per * n + per)
                plain(pool)
                nc.gpsimd.tensor_scalar(mid[:, :], var, EPS, None, ALU.add).then_inc(mid_sem, 1)
                pool.wait_ge(mid_sem, n + 1)
                nc.gpsimd.tensor_tensor(dst[:, :], mid[:, :], neg_half[:, :], ALU.pow).then_inc(dst_sem, 1)

            def ln1(b):
                inverse(b, s_stat, NTOK, mv[:, :, 1], veps, s_veps, rstd, s_rstd)

            def step(s, par):
                proj, attend, finish = doing(s)
                if isinstance(s, int) and s == 0:
                    ln1(0)
                if not isinstance(s, int) or s + 1 < B:
                    ln1(s + 1)
                if finish:
                    b = s - 2
                    inverse(b, s_cstat, NTOK, cmv[:, :, 1], cveps, s_cveps, crstd, s_crstd)
                    for j in range(NTOK):
                        pool.wait_ge(s_cln, b * NTOK + j + 1)
                        nc.gpsimd.tensor_tensor(xs[:, b, j, :], xs[:, b, j, :], ctxn[:, j, :], ALU.add)\
                          .then_inc(s_x1, 1)

            steps(pool, step)


def constants():
    import numpy as np
    q = np.zeros((N_MASK + N_MAX, 8 * BLK), np.float32)
    k = np.zeros((N_MASK + N_MAX, 8 * BLK), np.float32)
    for r, (left, right) in enumerate(HOLES):
        for pos, blk in enumerate(ORDER):
            cols = slice(pos * BLK, (pos + 1) * BLK)
            if blk in left:
                q[r, cols] = 1.0
            if blk in right:
                k[r, cols] = -BIG
    k[N_MASK:] = -1.0
    return q, k, np.eye(P, dtype=np.float32)


NE = 8
TOPK = 2
RT = 256
NROT = 3



def routed_sizes(tokens):
    region = tokens + RT
    tiles = (TOPK * tokens + NE * (RT - 1)) // RT
    return region, tiles + tiles % 2


def ffn_constants(tokens):
    import numpy as np
    region, tiles = routed_sizes(tokens)
    before = np.triu(np.ones((P, P), np.float32), 1)
    wide = np.concatenate([np.arange(NE), np.arange(NE) * region, np.arange(tiles)]).astype(np.float32)
    return np.concatenate([np.eye(P, dtype=np.float32), before, np.broadcast_to(wide, (P, wide.size))], 1)


def ffn(nc, xs, w, out):
    _, B, NTOK, D = xs.shape
    KC = D // P
    TILES = B * NTOK
    TOKENS = TILES * P
    F = w["ew1"].shape[2]
    FC = F // P
    REGION, RTILES = routed_sizes(TOKENS)
    RB = RT // P
    HALVINGS = B // 2

    ctx = ExitStack()
    with ctx:
        def sb(name, shape, dt=F32, where=ctx):
            return where.enter_context(nc.sbuf_tensor(name, shape, dt))

        def sem(name):
            return ctx.enter_context(nc.semaphore(name))

        def wait(eng, s, value):
            if not isinstance(value, int) or value > 0:
                eng.wait_ge(s, value)

        def plain(eng):
            eng.nop(nofuse=True)

        z_rows = nc.dram_tensor("z_rows", [NE * REGION, D], F32, kind="Internal").ap()
        y_rows = nc.dram_tensor("y_rows", [RTILES * RT, D], F32, kind="Internal").ap()
        abel_rows = nc.dram_tensor("abel_rows", [TILES * P, D], F32, kind="Internal").ap()
        eb2_spill = nc.dram_tensor("eb2_spill", [NE, D], F32, kind="Internal").ap()

        w1 = sb("w1", [P, NE, KC, F])
        w2 = sb("w2", [P, NE, FC, D])
        b1 = sb("b1", [P, NE, FC])
        b2 = sb("b2", [P, NE, D])
        cst = sb("cst", [P, 2 * P + 2 * NE + RTILES])
        ident, numbers = cst[:, 0:P], cst[:, 2 * P:2 * P + NE]
        first_row, tile_no = cst[:, 2 * P + NE:2 * P + 2 * NE], cst[:, 2 * P + 2 * NE:]
        affine = sb("affine", [P, 2, KC])
        mv1 = sb("mv1", [P, TILES, 2])
        rstd1 = sb("rstd1", [P, TILES])
        region_row = sb("region_row", [P, TILES, TOPK])
        result_row = sb("result_row", [P, TILES, TOPK], U32)
        top = sb("top", [P, TILES, TOPK])
        neg_half = sb("neg_half2", [P, NTOK])
        table = sb("table", [P, 2, RTILES], I32)
        tail = sb("tail", [P, NE], I32)

        g_load = sem("g_load")
        g_weights = sem("g_weights")
        g_first = sem("g_first")
        g_table = sem("g_table")

        gate_ctx = ExitStack()
        with gate_ctx:
            def gsb(name, shape, dt=F32):
                return sb(name, shape, dt, gate_ctx)

            wab = gsb("wab", [P, KC, D + NE])
            bias_ab = gsb("bias_ab", [P, D + NE])
            before = gsb("before", [P, P], BF16)
            ones = gsb("ones", [P, P], BF16)
            y = gsb("y", [P, NTOK, D])
            z = [gsb(f"z{i}", [P, NTOK, D]) for i in range(2)]
            mv0 = gsb("mv0", [P, NTOK, 2])
            st1 = gsb("st1", [P, NTOK, 6])
            st2 = gsb("st2", [P, NTOK, 6])
            mv2 = gsb("mv2", [P, NTOK, 2])
            ve = gsb("ve", [P, 2, NTOK])
            rstd2 = gsb("rstd2", [P, NTOK])
            zT = gsb("zT", [P, KC, NTOK * P])
            pre = gsb("pre", [P, NTOK, D])
            abel = gsb("abel", [P, NTOK, D])
            logit = gsb("logit", [P, NTOK, NE])
            best = gsb("best", [P, NTOK, NE])
            best_i = gsb("best_i", [P, NTOK, NE], U32)
            best_f = gsb("best_f", [P, TOPK, NTOK])
            hot = gsb("hot", [P, TOPK, NTOK, NE])
            chosen = gsb("chosen", [P, NTOK, NE], BF16)
            batch_sum = gsb("batch_sum", [P, NE])
            carry = [gsb(f"carry{i}", [P, NE], BF16) for i in range(2)]
            place = gsb("place", [P, NTOK, NE])
            pick = gsb("pick", [P, TOPK, NTOK, NE])
            dest_f = gsb("dest_f", [P, TOPK, NTOK])
            to_row = [gsb(f"to_row{i}", [P, NTOK, TOPK], U32) for i in range(2)]
            gA = gsb("gA", [P, NROT, KC, D])
            gAT = gsb("gAT", [P, NROT, KC, D])
            gE = gsb("gE", [P, NROT, KC, D])
            gET = gsb("gET", [P, NROT, KC, D])
            prod = gAT
            w2T = [gsb(f"w2T{i}", [P, KC, F]) for i in range(2)]
            eb2T = gsb("eb2T", [P, KC, NE])
            eb2_out = gsb("eb2_out", [NE, D])
            tb = gsb("tb", [P, 5, RTILES])
            cnt = gsb("cnt", [P, 6, NE])
            cnt_i = gsb("cnt_i", [P, 2, NE], I32)
            zero = gsb("zero", [P, RB, D])
            shift = gsb("shift", [P, 2, TILES * TOPK])

            def bank(name):
                return gate_ctx.enter_context(nc.psum_tensor(name, [P, 512], F32))

            zt_ps = [bank(f"zt_ps{k}") for k in range(KC)]
            ab_ps = [bank(f"ab_ps{k}") for k in range(2)]
            lg_ps = bank("lg_ps")
            LG, PL = lg_ps[:, 0:NTOK * NE], lg_ps[:, 64:64 + NTOK * NE]
            rot_ps = [bank(f"rot_ps{k}") for k in range(NROT)]

            g_st = sem("g_st")
            g_mv = sem("g_mv")
            g_mv1 = sem("g_mv1")
            g_ve = sem("g_ve")
            g_rs = sem("g_rs")
            g_y = sem("g_y")
            g_st2 = sem("g_st2")
            g_mv2 = sem("g_mv2")
            g_ve2 = sem("g_ve2")
            g_rs2 = sem("g_rs2")
            g_z = sem("g_z")
            g_scat = [sem(f"g_scat{i}") for i in range(2)]
            g_zt = sem("g_zt")
            g_ztc = sem("g_ztc")
            g_ab = sem("g_ab")
            g_lg = sem("g_lg")
            g_pre = sem("g_pre")
            g_log = sem("g_log")
            g_abel = sem("g_abel")
            g_abst = sem("g_abst")
            g_best = sem("g_best")
            g_bi = sem("g_bi")
            g_bf = sem("g_bf")
            g_hot = sem("g_hot")
            g_chosen = sem("g_chosen")
            g_bsum = sem("g_bsum")
            g_carry = sem("g_carry")
            g_pl = sem("g_pl")
            g_place = sem("g_place")
            g_pick = sem("g_pick")
            g_df = sem("g_df")
            g_dest = sem("g_dest")
            g_top = sem("g_top")
            g_kept = sem("g_kept")
            g_init = sem("g_init")
            r_full = [sem(f"r_full{i}") for i in range(NROT)]
            r_free = [sem(f"r_free{i}") for i in range(NROT)]
            r_load = sem("r_load")
            r_v = sem("r_v")
            r_w2 = [sem(f"r_w2{i}") for i in range(2)]
            r_eb = sem("r_eb")
            g_tail = sem("g_tail")
            g_exp = sem("g_exp")
            g_t = sem("g_t")

            block = gate_ctx.enter_context(nc.Block())

            def steps(eng, step):
                for s in range(2):
                    step(s, s % 2, s // 2)
                with eng.Fori(1, B // 2 - 1) as i:
                    step(2 * i, 0, i)
                    step(2 * i + 1, 1, i)
                for s in range(B - 2, B + 1):
                    step(s, s % 2, s // 2)

            def has(s, batch):
                return not isinstance(s, int) or 0 <= batch < B

            SERIES = [6, 30, 120, 360, 720]
            PREP = len(SERIES) + 1
            R_SERIES = 3
            R_PLUS = R_SERIES + 4
            T_DIFF = 1

            def ROT_END(i):
                return PREP + 2 * HALVINGS + (3 if i == 0 else 0)


            @block.sync
            def _(sp):
                sp.dma_start(cst[:, :], w["consts"]).then_inc(g_load, 16)
                sp.dma_start(wab[:, :, :], w["wab"].rearrange("(k p) n -> p k n", p=P)).then_inc(g_load, 16)
                sp.dma_start(bias_ab[:, :], w["bias_ab"]).then_inc(g_load, 16)
                sp.dma_start(affine[:, :, :], w["affine"]).then_inc(g_load, 16)
                for i in range(NROT):
                    sp.dma_start(gA[:, i, :, :], w["gens"][i].rearrange("(k p) n -> p k n", p=P)).then_inc(r_load, 16)
                    sp.dma_start(gAT[:, i, :, :], w["gensT"][i].rearrange("(k p) n -> p k n", p=P)).then_inc(r_load, 16)
                sp.dma_start(eb2T[:, :, :], w["eb2T"].rearrange("(k p) e -> p k e", p=P)).then_inc(r_load, 16)
                sp.dma_start(b1[:, :, :], w["eb1"]).then_inc(g_weights, 16)
                for e in range(2):
                    sp.dma_start(w2T[e][:, :, :], w["ew2T"][e].rearrange("(k p) f -> p k f", p=P)).then_inc(r_w2[e], 16)
                for e in range(NE):
                    sp.dma_start(w1[:, e, :, :], w["ew1"][e].rearrange("(k p) f -> p k f", p=P)).then_inc(g_weights, 16)

                def step(s, par, turn):
                    if has(s, s - 1 if isinstance(s, int) else s):
                        b = s - 1
                        sp.wait_ge(g_abel, b + 1)
                        dst = abel_rows.rearrange("(b j p) d -> b p j d", j=NTOK, p=P)
                        sp.dma_start(dst[b], abel[:, :, :]).then_inc(g_abst, 16)

                steps(sp, step)
                for e in range(2, NE):
                    sp.wait_ge(r_full[e % 2], ROT_END(e % 2) + (e // 2) * FC // 2)
                    sp.dma_start(w2T[e % 2][:, :, :], w["ew2T"][e].rearrange("(k p) f -> p k f", p=P))\
                      .then_inc(r_w2[e % 2], 16)
                sp.wait_ge(r_eb, 1)
                sp.dma_start(eb2_spill, eb2_out[:, :]).then_inc(g_tail, 16)
                sp.wait_ge(g_tail, 16)
                sp.dma_start(b2[:, :, :], eb2_spill.rearrange("(o e) d -> o e d", o=1).broadcast_to([P, NE, D])).then_inc(g_tail, 16)
                sp.wait_ge(g_table, 1)
                for e in range(NE):
                    row = sp.value_load(tail[0:1, e:e + 1], min_val=e * REGION, max_val=e * REGION + TOKENS)
                    sp.dma_start(z_rows[bass.ds(row, RT), :].rearrange("(r p) d -> p r d", p=P), zero[:, :, :])\
                      .then_inc(g_tail, 16)
                sp.wait_ge(g_tail, 16 * (2 + NE))
                sp.wait_ge(g_abst, 16 * B)
                sp.wait_ge(g_weights, 16 * (1 + NE))

            @block.tensor
            def _(pe):
                pe.wait_ge(g_load, 4 * 16)
                pe.wait_ge(g_init, 6)

                def product(i, n, lhsT, rhs):
                    pe.wait_ge(r_free[i], n)
                    for m in range(KC):
                        for k in range(KC):
                            ins = nc.tensor.matmul(rot_ps[i][:, m * D:(m + 1) * D], lhsT[:, k, m * P:(m + 1) * P],
                                                   rhs[:, k, :], start=(k == 0), stop=(k == KC - 1))
                    ins.then_inc(r_full[i], 1)

                def turned(i, n, src):
                    pe.wait_ge(r_free[i], n)
                    for m in range(KC):
                        for k in range(KC):
                            ins = nc.tensor.transpose(rot_ps[i][:, m * D + k * P:m * D + (k + 1) * P],
                                                      src[:, k, m * P:(m + 1) * P], ident)
                    ins.then_inc(r_full[i], 1)

                pe.wait_ge(r_v, 2)
                for n in range(len(SERIES)):
                    for i in range(NROT):
                        product(i, n, gAT[:, i], (gE if n else gA)[:, i])
                pe.wait_ge(r_v, R_SERIES)
                for i in range(NROT):
                    turned(i, len(SERIES), gE[:, i])

                def gate(b):
                    for k in range(KC):
                        pe.wait_ge(g_ztc, b * KC + k)
                        for j in range(NTOK):
                            pe.wait_ge(g_z, b * NTOK + j + 1)
                            ins = nc.tensor.transpose(zt_ps[k][:, j * P:(j + 1) * P], z_of(b)[:, j, k * P:(k + 1) * P], ident)
                        ins.then_inc(g_zt, 1)

                def dense(b):
                    pe.wait_ge(g_ztc, (b + 1) * KC)
                    pe.wait_ge(g_pre, b * 2)
                    for j in range(NTOK):
                        for k in range(KC):
                            ins = nc.tensor.matmul(ab_ps[j // 2][:, j % 2 * D:(j % 2 + 1) * D],
                                                   zT[:, k, j * P:(j + 1) * P], wab[:, k, 0:D],
                                                   start=(k == 0), stop=(k == KC - 1))
                        if j % 2:
                            ins.then_inc(g_ab, 1)
                    pe.wait_ge(g_log, b)
                    for j in range(NTOK):
                        for k in range(KC):
                            ins = nc.tensor.matmul(LG[:, j * NE:(j + 1) * NE], zT[:, k, j * P:(j + 1) * P],
                                                   wab[:, k, D:D + NE], start=(k == 0), stop=(k == KC - 1))
                    ins.then_inc(g_lg, 1)

                def ranks(b, par):
                    pe.wait_ge(g_chosen, b + 1)
                    wait(pe, g_carry, b)
                    wait(pe, g_place, b)
                    v = chosen[:, :, :].rearrange("p j e -> p (j e)")
                    nc.tensor.matmul(PL, before[:, :], v, start=True, stop=False)
                    c = carry[par][:, :].rearrange("p (o e) -> p o e", o=1)
                    nc.tensor.matmul(PL, ones[:, :], c.broadcast_to([P, NTOK, NE]), start=False, stop=False)
                    for j in range(NTOK - 1):
                        n = NTOK - 1 - j
                        src = chosen[:, j:j + 1, :].broadcast_to([P, n, NE])
                        ins = nc.tensor.matmul(PL[:, (j + 1) * NE:NTOK * NE], ones[:, :], src,
                                               start=False, stop=(n == 1))
                    ins.then_inc(g_pl, 1)

                def square(turn):
                    n = PREP + 2 * turn
                    for i in range(NROT):
                        product(i, n, gET[:, i], gE[:, i])
                    for i in range(NROT):
                        turned(i, n + 1, gE[:, i])

                z_now = [None]

                def z_of(b):
                    return z_now[0]

                def step(s, par, turn):
                    if has(s, s):
                        z_now[0] = z[par]
                        gate(s)
                        dense(s)
                        if par:
                            square(turn)
                    if has(s, s - 1 if isinstance(s, int) else s):
                        ranks(s - 1, 1 - par)

                steps(pe, step)

                n = PREP + 2 * HALVINGS
                pe.wait_ge(r_v, R_PLUS)
                product(0, n, gET[:, 0], gE[:, 1])
                turned(0, n + 1, prod[:, 0])
                product(0, n + 2, prod[:, 1], gE[:, 2])
                for e in range(NE):
                    i = e % 2
                    if e < 2:
                        pe.wait_ge(r_free[0], n + 3)
                    pe.wait_ge(r_w2[i], 16 * (e // 2 + 1))
                    for half in range(FC // 2):
                        use = ROT_END(i) + (e // 2) * (FC // 2) + half
                        pe.wait_ge(r_free[i], use)
                        for f in range(2):
                            c = (half * 2 + f) * P
                            for k in range(KC):
                                ins = nc.tensor.matmul(rot_ps[i][:, f * D:(f + 1) * D], w2T[i][:, k, c:c + P],
                                                       prod[:, 2, k, :], start=(k == 0), stop=(k == KC - 1))
                        ins.then_inc(r_full[i], 1)
                for k in range(KC):
                    ins = nc.tensor.matmul(rot_ps[2][0:NE, 0:D], eb2T[:, k, :], prod[:, 2, k, :],
                                           start=(k == 0), stop=(k == KC - 1))
                ins.then_inc(r_full[2], 1)
                pe.wait_ge(g_carry, B)
                pe.wait_ge(g_place, B)
                nc.tensor.matmul(PL[:, 0:NE], ones[:, :], carry[B % 2][:, :], start=True, stop=True).then_inc(g_pl, 1)


            @block.scalar
            def _(act):
                act.wait_ge(g_load, 4 * 16)

                def copy_rot(i, n, dst):
                    act.wait_ge(r_full[i], n + 1)
                    nc.scalar.copy(dst, rot_ps[i][:, :].rearrange("p (k d) -> p k d", d=D)).then_inc(r_free[i], 1)

                for i in range(NROT):
                    copy_rot(i, len(SERIES), gET[:, i])

                def step(s, par, turn):
                    if has(s, s):
                        b = s
                        for k in range(KC):
                            act.wait_ge(g_zt, b * KC + k + 1)
                            if k == 0:
                                act.wait_ge(g_lg, b)
                            nc.scalar.activation(zT[:, k, :], zt_ps[k][:, :], ACT.Identity,
                                                 scale=affine[:, 0, k:k + 1], bias=affine[:, 1, k:k + 1])\
                              .then_inc(g_ztc, 1)
                        if par:
                            n = PREP + 2 * turn
                            for i in range(NROT):
                                copy_rot(i, n + 1, gET[:, i])
                    if has(s, s - 1 if isinstance(s, int) else s):
                        b = s - 1
                        act.wait_ge(g_pre, (b + 1) * 2)
                        act.wait_ge(g_abst, b * 16)
                        nc.scalar.activation(abel[:, :, :], pre[:, :, :], ACT.Gelu).then_inc(g_abel, 1)

                steps(act, step)
                n = PREP + 2 * HALVINGS
                for m in range(3):
                    copy_rot(0, n + m, prod[:, m])
                for e in range(NE):
                    i = e % 2
                    for half in range(FC // 2):
                        copy_rot(i, ROT_END(i) + (e // 2) * (FC // 2) + half, w2[:, e, 2 * half:2 * half + 2, :])
                act.wait_ge(r_full[2], ROT_END(2) + 1)
                nc.scalar.copy(eb2_out[:, :], rot_ps[2][0:NE, 0:D]).then_inc(r_eb, 1)
                act.wait_ge(g_t, T_DIFF)
                nc.scalar.activation(top[:, :, 1], top[:, :, 1], ACT.Exp).then_inc(g_exp, 1)

            @block.vector
            def _(dve):
                nc.vector.memset(ones[:, :], 1.0).then_inc(g_init, 1)
                nc.vector.memset(neg_half[:, :], -0.5).then_inc(g_init, 1)
                for i in range(2):
                    nc.vector.memset(carry[i][:, :], 0.0).then_inc(g_init, 1)
                nc.vector.memset(zero[:, :, :], 0.0).then_inc(g_init, 1)
                dve.wait_ge(g_load, 4 * 16)
                nc.vector.tensor_copy(before[:, :], cst[:, P:2 * P]).then_inc(g_init, 1)
                dve.wait_ge(r_load, (2 * NROT + 1) * 16)
                nc.vector.tensor_scalar(gA[:, :, :, :], gA[:, :, :, :], 0.5 ** HALVINGS, None, ALU.mult).then_inc(r_v, 1)
                nc.vector.tensor_scalar(gAT[:, :, :, :], gAT[:, :, :, :], 0.5 ** HALVINGS, None, ALU.mult).then_inc(r_v, 1)
                dve.wait_ge(r_v, 2)

                def rot(i):
                    return rot_ps[i][:, :].rearrange("p (k d) -> p k d", d=D)

                for n, c in enumerate(SERIES):
                    for i in range(NROT):
                        dve.wait_ge(r_full[i], n + 1)
                        nc.vector.scalar_tensor_tensor(out=gE[:, i], in0=gA[:, i], scalar=float(c), in1=rot(i),
                                                       op0=ALU.mult, op1=ALU.add).then_inc(r_free[i], 1)
                for i in range(NROT):
                    dve.wait_ge(r_free[i], len(SERIES))
                nc.vector.tensor_scalar(gE[:, :, :, :], gE[:, :, :, :], 1.0 / SERIES[-1], None, ALU.mult).then_inc(r_v, 1)

                def stats(b):
                    wait(dve, g_mv, b * NTOK)
                    for j in range(NTOK):
                        nc.vector.bn_stats(st1[:, j, :], xs[:, b, j, :]).then_inc(g_st, 1)
                    dve.wait_ge(g_st, (b + 1) * NTOK)
                    wait(dve, g_mv1, b)
                    plain(dve)
                    for j in range(NTOK):
                        nc.vector.bn_aggr(mv0[:, j, :], st1[:, j, :]).then_inc(g_mv, 1)
                    dve.wait_ge(g_mv, (b + 1) * NTOK)
                    nc.vector.tensor_copy(mv1[:, bass.ds(b * NTOK, NTOK), :], mv0[:, :, :]).then_inc(g_mv1, 1)

                def norm_y(b):
                    dve.wait_ge(g_rs, b + 1)
                    wait(dve, g_z, b * NTOK)
                    for j in range(NTOK):
                        t = b * NTOK + j
                        nc.vector.tensor_scalar(y[:, j, :], xs[:, b, j, :], mv0[:, j, 0:1], rstd1[:, bass.ds(t, 1)],
                                                ALU.subtract, ALU.mult).then_inc(g_y, 1)
                    for j in range(NTOK):
                        dve.wait_ge(g_y, b * NTOK + j + 1)
                        nc.vector.bn_stats(st2[:, j, :], y[:, j, :]).then_inc(g_st2, 1)
                    dve.wait_ge(g_st2, (b + 1) * NTOK)
                    plain(dve)
                    for j in range(NTOK):
                        nc.vector.bn_aggr(mv2[:, j, :], st2[:, j, :]).then_inc(g_mv2, 1)

                def norm_z(b, par, turn):
                    dve.wait_ge(g_rs2, b + 1)
                    dve.wait_ge(g_scat[par], turn * NTOK * TOPK * 16)
                    for j in range(NTOK):
                        nc.vector.tensor_scalar(z[par][:, j, :], y[:, j, :], mv2[:, j, 0:1], rstd2[:, j:j + 1],
                                                ALU.subtract, ALU.mult).then_inc(g_z, 1)

                def route(b):
                    wait(dve, g_kept, b)
                    dve.wait_ge(g_abel, b)
                    bias = bias_ab[:, 0:D].rearrange("p (o d) -> p o d", o=1).broadcast_to([P, 2, D])
                    for n in range(2):
                        dve.wait_ge(g_ab, b * 2 + n + 1)
                        nc.vector.tensor_tensor(pre[:, 2 * n:2 * n + 2, :],
                                                ab_ps[n][:, :].rearrange("p (j d) -> p j d", d=D), bias, ALU.add)\
                          .then_inc(g_pre, 1)
                    dve.wait_ge(g_lg, b + 1)
                    gbias = bias_ab[:, D:D + NE].rearrange("p (o e) -> p o e", o=1).broadcast_to([P, NTOK, NE])
                    nc.vector.tensor_tensor(logit[:, :, :], LG.rearrange("p (j e) -> p j e", e=NE), gbias, ALU.add)\
                      .then_inc(g_log, 1)
                    dve.wait_ge(g_log, b + 1)
                    plain(dve)
                    for j in range(NTOK):
                        nc.vector.max(best[:, j, :], logit[:, j, :]).then_inc(g_best, 1)
                    dve.wait_ge(g_best, (b + 1) * NTOK)
                    plain(dve)
                    for j in range(NTOK):
                        nc.vector.max_index(best_i[:, j, :], best[:, j, :], logit[:, j, :]).then_inc(g_bi, 1)
                    nc.vector.tensor_copy(top[:, bass.ds(b * NTOK, NTOK), :], best[:, :, 0:TOPK]).then_inc(g_top, 1)
                    dve.wait_ge(g_bi, (b + 1) * NTOK)
                    nc.vector.tensor_copy(best_f[:, :, :], best_i[:, :, 0:TOPK].rearrange("p j s -> p s j"))\
                      .then_inc(g_bf, 1)
                    dve.wait_ge(g_bf, b + 1)
                    iota = numbers.rearrange("p (o e) -> p o e", o=1).broadcast_to([P, NTOK, NE])
                    for s in range(TOPK):
                        mine = best_f[:, s, :].rearrange("p (j o) -> p j o", o=1).broadcast_to([P, NTOK, NE])
                        nc.vector.tensor_tensor(hot[:, s, :, :], iota, mine, ALU.is_equal).then_inc(g_hot, 1)
                    dve.wait_ge(g_hot, (b + 1) * TOPK)
                    dve.wait_ge(g_pl, b)
                    nc.vector.tensor_tensor(chosen[:, :, :], hot[:, 0, :, :], hot[:, 1, :, :], ALU.add)\
                      .then_inc(g_chosen, 1)

                def count(b, par):
                    dve.wait_ge(g_chosen, b + 1)
                    nc.vector.tensor_reduce(batch_sum[:, :], chosen[:, :, :].rearrange("p j e -> p e j"), AX_X, ALU.add)\
                      .then_inc(g_bsum, 1)
                    dve.wait_ge(g_bsum, b + 1)
                    nc.vector.tensor_tensor(carry[1 - par][:, :], carry[par][:, :], batch_sum[:, :], ALU.add)\
                      .then_inc(g_carry, 1)

                def destinations(b, par):
                    dve.wait_ge(g_pl, b + 1)
                    off = first_row.rearrange("p (o e) -> p o e", o=1).broadcast_to([P, NTOK, NE])
                    nc.vector.tensor_tensor(place[:, :, :], PL.rearrange("p (j e) -> p j e", e=NE), off, ALU.add)\
                      .then_inc(g_place, 1)
                    dve.wait_ge(g_place, b + 1)
                    for s in range(TOPK):
                        nc.vector.tensor_tensor(pick[:, s, :, :], hot[:, s, :, :], place[:, :, :], ALU.mult)\
                          .then_inc(g_pick, 1)
                    dve.wait_ge(g_pick, (b + 1) * TOPK)
                    nc.vector.tensor_reduce(dest_f[:, :, :], pick[:, :, :, :], AX_X, ALU.add).then_inc(g_df, 1)
                    dve.wait_ge(g_df, b + 1)
                    nc.vector.tensor_copy(to_row[par][:, :, :], dest_f[:, :, :].rearrange("p s j -> p j s"))\
                      .then_inc(g_dest, 1)
                    nc.vector.tensor_copy(region_row[:, bass.ds(b * NTOK, NTOK), :],
                                          dest_f[:, :, :].rearrange("p s j -> p j s")).then_inc(g_kept, 1)

                def square(turn):
                    n = PREP + 2 * turn
                    for i in range(NROT):
                        dve.wait_ge(r_full[i], n + 1)
                        nc.vector.scalar_tensor_tensor(out=gE[:, i], in0=gE[:, i], scalar=2.0, in1=rot(i),
                                                       op0=ALU.mult, op1=ALU.add).then_inc(r_free[i], 1)

                stats(0)

                def step(s, par, turn):
                    if has(s, s):
                        norm_y(s)
                        if has(s, s + 1 if isinstance(s, int) else s):
                            stats(s + 1)
                        norm_z(s, par, turn)
                    if has(s, s - 1 if isinstance(s, int) else s):
                        route(s - 1)
                        count(s - 1, 1 - par)
                    if has(s, s) and par:
                        square(turn)
                    if has(s, s - 1 if isinstance(s, int) else s):
                        destinations(s - 1, 1 - par)

                steps(dve, step)

                chain = [0]

                def link(ins):
                    chain[0] += 1
                    ins.then_inc(g_t, 1)
                    dve.wait_ge(g_t, chain[0])
                    return chain[0]

                for i in range(NROT):
                    dve.wait_ge(r_free[i], PREP + 2 * HALVINGS)
                for dst in (gE[:, 0], gE[:, 1], gE[:, 2], gET[:, 0]):
                    for k in range(KC):
                        d = dst[:, k, k * P:(k + 1) * P]
                        ins = nc.vector.tensor_tensor(d, d, ident, ALU.add)
                    ins.then_inc(r_v, 1)

                dve.wait_ge(g_top, B)
                dve.wait_ge(g_kept, B)
                at = link(nc.vector.tensor_tensor(top[:, :, 1], top[:, :, 1], top[:, :, 0], ALU.subtract))
                assert at == T_DIFF
                dve.wait_ge(g_exp, 1)
                link(nc.vector.tensor_scalar(top[:, :, 0], top[:, :, 1], 1.0, None, ALU.add))
                link(nc.vector.reciprocal(top[:, :, 0], top[:, :, 0]))
                link(nc.vector.tensor_tensor(top[:, :, 1], top[:, :, 1], top[:, :, 0], ALU.mult))

                dve.wait_ge(g_pl, B + 1)
                count_f, tiles_f, upto = cnt[:, 0, :], cnt[:, 1, :], cnt[:, 2, :]
                link(nc.vector.tensor_copy(count_f, PL[:, 0:NE]))
                link(nc.vector.tensor_tensor(cnt[:, 3, :], count_f, first_row, ALU.add))
                link(nc.vector.tensor_copy(tail[:, :], cnt[:, 3, :]))
                link(nc.vector.tensor_scalar(cnt[:, 4, :], count_f, float(RT - 1), None, ALU.add))
                link(nc.vector.tensor_copy(cnt_i[:, 0, :], cnt[:, 4, :]))
                link(nc.vector.tensor_scalar(cnt_i[:, 1, :], cnt_i[:, 0, :], RT.bit_length() - 1, None,
                                             ALU.arith_shift_right))
                link(nc.vector.tensor_copy(tiles_f, cnt_i[:, 1, :]))
                link(nc.vector.tensor_copy(upto, tiles_f))
                for e in range(1, NE):
                    link(nc.vector.tensor_tensor(upto[:, e:e + 1], upto[:, e - 1:e], tiles_f[:, e:e + 1], ALU.add))
                no, exp_, start, row, live = (tb[:, n, :] for n in range(5))
                link(nc.vector.tensor_scalar(cnt[:, 5, 0:1], upto[:, NE - 1:NE], -1.0, None, ALU.add))
                link(nc.vector.tensor_scalar(no, tile_no, cnt[:, 5, 0:1], None, ALU.min))
                link(nc.vector.tensor_scalar(exp_, no, upto[:, 0:1], None, ALU.is_ge))
                link(nc.vector.tensor_scalar(start, exp_, tiles_f[:, 0:1], None, ALU.mult))
                for e in range(1, NE - 1):
                    link(nc.vector.tensor_scalar(live, no, upto[:, e:e + 1], None, ALU.is_ge))
                    link(nc.vector.tensor_tensor(exp_, exp_, live, ALU.add))
                    link(nc.vector.scalar_tensor_tensor(out=start, in0=live, scalar=tiles_f[:, e:e + 1], in1=start,
                                                        op0=ALU.mult, op1=ALU.add))
                link(nc.vector.tensor_tensor(row, no, start, ALU.subtract))
                link(nc.vector.tensor_scalar(row, row, float(RT), None, ALU.mult))
                link(nc.vector.scalar_tensor_tensor(out=row, in0=exp_, scalar=float(REGION), in1=row,
                                                    op0=ALU.mult, op1=ALU.add))
                link(nc.vector.tensor_copy(table[:, 0, :], exp_))
                link(nc.vector.tensor_copy(table[:, 1, :], row))
                step_e = cnt[:, 3, :]
                link(nc.vector.tensor_scalar(step_e, tiles_f, float(RT), float(-REGION), ALU.mult, ALU.add))
                flat = region_row[:, :, :].rearrange("p t s -> p (t s)")
                moved = shift[:, 0, :]
                link(nc.vector.tensor_copy(moved, flat))
                for e in range(1, NE):
                    link(nc.vector.tensor_scalar(shift[:, 1, :], flat, first_row[:, e:e + 1], step_e[:, e - 1:e],
                                                 ALU.is_ge, ALU.mult))
                    link(nc.vector.tensor_tensor(moved, moved, shift[:, 1, :], ALU.add))
                nc.vector.tensor_copy(result_row[:, :, :].rearrange("p t s -> p (t s)"), moved).then_inc(g_table, 1)

            @block.gpsimd
            def _(pool):
                pool.wait_ge(g_init, 6)

                def inverse(ready, want, n, var, dst, mid_sem, dst_sem):
                    pool.wait_ge(ready, want)
                    plain(pool)
                    m = ve[:, 0 if mid_sem is g_ve else 1, :]
                    nc.gpsimd.tensor_scalar(m, var, EPS, None, ALU.add).then_inc(mid_sem, 1)
                    pool.wait_ge(mid_sem, n + 1)
                    nc.gpsimd.tensor_tensor(dst, m, neg_half[:, :], ALU.pow).then_inc(dst_sem, 1)

                def inverse1(b):
                    inverse(g_mv, (b + 1) * NTOK, b, mv0[:, :, 1],
                            rstd1[:, bass.ds(b * NTOK, NTOK)], g_ve, g_rs)

                inverse1(0)

                def step(s, par, turn):
                    if has(s, s):
                        inverse(g_mv2, (s + 1) * NTOK, s, mv2[:, :, 1], rstd2[:, :], g_ve2, g_rs2)
                        if has(s, s + 1 if isinstance(s, int) else s):
                            inverse1(s + 1)
                    if has(s, s - 1 if isinstance(s, int) else s):
                        b = s - 1
                        pool.wait_ge(g_dest, b + 1)
                        plain(pool)
                        for j in range(NTOK):
                            for k in range(TOPK):
                                idx = to_row[1 - par][:, j, k:k + 1]
                                pool.indirect_dma_start(z_rows, bass.IndirectOffsetOnAxis(ap=idx, axis=0),
                                                        z[1 - par][:, j, :], None)\
                                    .then_inc(g_scat[1 - par], 16)

                steps(pool, step)
                for i in range(2):
                    pool.wait_ge(g_scat[i], (B // 2) * NTOK * TOPK * 16)

        exp_ctx = ExitStack()
        with exp_ctx:
            def esb(name, shape, dt=F32):
                return sb(name, shape, dt, exp_ctx)

            rows_in = [esb(f"rows_in{i}", [P, RB, D]) for i in range(2)]
            w1c = [esb(f"w1c{i}", [P, KC, F]) for i in range(2)]
            b1c = [esb(f"b1c{i}", [P, FC]) for i in range(2)]
            inT = esb("inT", [P, KC, RT])
            hT = esb("hT", [P, FC, RT])
            rows_out = [esb(f"rows_out{i}", [P, RB, D]) for i in range(2)]

            def ebank(name):
                return exp_ctx.enter_context(nc.psum_tensor(name, [P, 512], F32))

            in_ps = [ebank(f"in_ps{i}") for i in range(2)]
            h_ps = [ebank(f"h_ps{i}") for i in range(4)]
            o_ps = [ebank(f"o_ps{i}") for i in range(2)]

            e_in = [sem(f"e_in{i}") for i in range(2)]
            e_w1 = sem("e_w1")
            e_b1 = sem("e_b1")
            e_turn_of = [sem(f"e_turn_of{i}") for i in range(2)]
            e_inT = sem("e_inT")
            e_h = sem("e_h")
            e_hT = sem("e_hT")
            e_o = sem("e_o")
            e_out = sem("e_out")
            e_store = [sem(f"e_store{i}") for i in range(2)]
            block = exp_ctx.enter_context(nc.Block())

            def turns(eng, tile):
                with eng.Fori(0, RTILES // 2) as i:
                    tile(2 * i, 0, i)
                    tile(2 * i + 1, 1, i)

            def lookup(eng, which, t, top_value):
                return eng.value_load(table[0:1, which, bass.ds(t, 1)], min_val=0, max_val=top_value)

            LAST = NE * REGION - RT

            @block.sync
            def _(sp):
                def tile(t, par, turn):
                    row = lookup(sp, 1, t, LAST)
                    sp.wait_ge(e_turn_of[par], turn)
                    sp.dma_start(rows_in[par][:, :, :], z_rows[bass.ds(row, RT), :].rearrange("(r p) d -> p r d", p=P))\
                      .then_inc(e_in[par], 16)

                turns(sp, tile)

            @block.scalar
            def _(act):
                def tile(t, par, turn):
                    act.wait_ge(e_b1, t + 1)
                    act.wait_ge(e_o, t)
                    for f in range(FC):
                        act.wait_ge(e_h, t * FC + f + 1)
                        nc.scalar.activation(hT[:, f, :], h_ps[f][:, 0:RT], ACT.Gelu, bias=b1c[par][:, f:f + 1])\
                          .then_inc(e_hT, 1)
                    act.wait_ge(e_out, t + 1)
                    act.dma_start(y_rows[bass.ds(t * RT, RT), :].rearrange("(r p) d -> p r d", p=P), rows_out[par][:, :, :])\
                       .then_inc(e_store[par], 16)

                turns(act, tile)
                for i in range(2):
                    act.wait_ge(e_store[i], 16 * (RTILES // 2))

            @block.tensor
            def _(pe):
                def turn_rows(t, par, turn):
                    pe.wait_ge(e_in[par], (turn + 1) * 16)
                    pe.wait_ge(e_inT, t * KC)
                    for k in range(KC):
                        for r in range(RB):
                            ins = nc.tensor.transpose(in_ps[k][:, r * P:(r + 1) * P],
                                                      rows_in[par][:, r, k * P:(k + 1) * P], ident)
                    ins.then_inc(e_turn_of[par], 1)

                def hidden(t, par):
                    pe.wait_ge(e_w1, t + 1)
                    pe.wait_ge(e_inT, (t + 1) * KC)
                    pe.wait_ge(e_hT, t * FC)
                    for f in range(FC):
                        for k in range(KC):
                            ins = nc.tensor.matmul(h_ps[f][:, 0:RT], w1c[par][:, k, f * P:(f + 1) * P], inT[:, k, :],
                                                   start=(k == 0), stop=(k == KC - 1))
                        ins.then_inc(e_h, 1)

                def result(t, e):
                    pe.wait_ge(e_out, t)
                    for r in range(RB):
                        for f in range(FC):
                            if r == 0:
                                pe.wait_ge(e_hT, t * FC + f + 1)
                            ins = nc.tensor.matmul(o_ps[0][:, r * D:(r + 1) * D], hT[:, f, r * P:(r + 1) * P],
                                                   w2[:, bass.ds(e, 1), f, :].rearrange("p o d -> p (o d)"),
                                                   start=(f == 0), stop=(f == FC - 1))
                    ins.then_inc(e_o, 1)

                def tile(t, par, turn):
                    turn_rows(t, par, turn)
                    hidden(t, par)
                    result(t, lookup(pe, 0, t, NE - 1))

                turns(pe, tile)

            @block.vector
            def _(dve):
                def tile(t, par, turn):
                    e = lookup(dve, 0, t, NE - 1)
                    dve.wait_ge(e_h, turn * 2 * FC)
                    nc.vector.tensor_copy(w1c[par][:, :, :], w1[:, bass.ds(e, 1), :, :].rearrange("p o k f -> p (o k) f"))\
                      .then_inc(e_w1, 1)
                    nc.vector.tensor_copy(b1c[par][:, :], b1[:, bass.ds(e, 1), :].rearrange("p o f -> p (o f)"))\
                      .then_inc(e_b1, 1)
                    for k in range(KC):
                        if k == 0:
                            dve.wait_ge(e_turn_of[par], turn + 1)
                            dve.wait_ge(e_h, t * FC)
                        nc.vector.tensor_scalar(inT[:, k, :], in_ps[k][:, 0:RT], affine[:, 0, k:k + 1],
                                                affine[:, 1, k:k + 1], ALU.mult, ALU.add).then_inc(e_inT, 1)
                    dve.wait_ge(e_o, t + 1)
                    dve.wait_ge(e_store[par], turn * 16)
                    nc.vector.tensor_tensor(rows_out[par][:, :, :], o_ps[0][:, :].rearrange("p (r d) -> p r d", d=D),
                                            b2[:, bass.ds(e, 1), :].broadcast_to([P, RB, D]), ALU.add).then_inc(e_out, 1)

                turns(dve, tile)

        fin_ctx = ExitStack()
        with fin_ctx:
            def fsb(name, shape, dt=F32):
                return sb(name, shape, dt, fin_ctx)

            rows = [fsb(f"rows{i}", [P, TOPK, NTOK, D]) for i in range(2)]
            ab = [fsb(f"ab{i}", [P, NTOK, D]) for i in range(2)]
            gcw = fsb("gcw", [P, 2, D])
            gcb = fsb("gcb", [P, 1])
            moe = fsb("moe", [P, NTOK, D])
            u = fsb("u", [P, NTOK, D])
            junk = fsb("junk", [P, D])
            dot = fsb("dot", [P, 2, NTOK])
            gl = fsb("gl", [P, 2, NTOK])
            fst = fsb("fst", [P, NTOK, 6])
            fmv = fsb("fmv", [P, NTOK, 2])
            fve = fsb("fve", [P, NTOK])
            frs = fsb("frs", [P, NTOK])
            o = [fsb(f"o{i}", [P, NTOK, D]) for i in range(2)]

            from_row = [fsb(f"from_row{i}", [P, NTOK, TOPK], U32) for i in range(2)]

            f_load = sem("f_load")
            f_idx = sem("f_idx")
            f_rows = [sem(f"f_rows{i}") for i in range(2)]
            f_ab = [sem(f"f_ab{i}") for i in range(2)]
            f_first = sem("f_first")
            f_free = sem("f_free")
            f_v = sem("f_v")
            f_x = sem("f_x")
            f_e = sem("f_e")
            f_mv = sem("f_mv")
            f_ve = sem("f_ve")
            f_rs = sem("f_rs")
            f_o = sem("f_o")
            f_out = [sem(f"f_out{i}") for i in range(2)]
            block = fin_ctx.enter_context(nc.Block())

            def pairs(eng, batch):
                with eng.Fori(0, B // 2) as i:
                    batch(2 * i, 0, i)
                    batch(2 * i + 1, 1, i)

            STEPS_V = 4 * NTOK + NTOK + 1 + 2 * NTOK

            @block.gpsimd
            def _(pool):
                def batch(b, par, turn):
                    pool.wait_ge(f_free, turn * 2)
                    nc.gpsimd.tensor_copy(from_row[par][:, :, :], result_row[:, bass.ds(b * NTOK, NTOK), :]).then_inc(f_idx, 1)
                    pool.wait_ge(f_idx, b + 1)
                    plain(pool)
                    for j in range(NTOK):
                        for k in range(TOPK):
                            idx = from_row[par][:, j, k:k + 1]
                            pool.indirect_dma_start(rows[par][:, k, j, :], None, y_rows,
                                                    bass.IndirectOffsetOnAxis(ap=idx, axis=0))\
                                .then_inc(f_rows[par], 16)
                    pool.wait_ge(f_mv, (b + 1) * NTOK)
                    plain(pool)
                    nc.gpsimd.tensor_scalar(fve[:, :], fmv[:, :, 1], EPS, None, ALU.add).then_inc(f_ve, 1)
                    pool.wait_ge(f_ve, b + 1)
                    nc.gpsimd.tensor_tensor(frs[:, :], fve[:, :], neg_half[:, :], ALU.pow).then_inc(f_rs, 1)

                pairs(pool, batch)

            @block.sync
            def _(sp):
                sp.dma_start(gcw[:, :, :], w["gcw"]).then_inc(f_load, 16)
                sp.dma_start(gcb[:, :], w["gcb"]).then_inc(f_load, 16)

                def batch(b, par, turn):
                    sp.wait_ge(f_free, turn * 2)
                    src = abel_rows.rearrange("(b j p) d -> b p j d", j=NTOK, p=P)
                    sp.dma_start(ab[par][:, :, :], src[b]).then_inc(f_ab[par], 16)

                pairs(sp, batch)

            @block.scalar
            def _(act):
                act.wait_ge(f_load, 32)

                def batch(b, par, turn):
                    act.wait_ge(f_x, b + 1)
                    nc.scalar.activation(gl[:, 1, :], gl[:, 0, :], ACT.Sigmoid).then_inc(f_e, 1)
                    act.wait_ge(f_o, (b + 1) * NTOK)
                    for pos, blk, n in RUNS:
                        lo = pos % 2 * BLK
                        act.dma_start(out[b, blk * BLK:(blk + n) * BLK, :], o[par][lo:lo + n * BLK, pos // 2, :])\
                           .then_inc(f_out[par], 16)

                pairs(act, batch)
                for i in range(2):
                    act.wait_ge(f_out[i], (B // 2) * len(RUNS) * 16)

            @block.vector
            def _(dve):
                dve.wait_ge(f_load, 32)

                def batch(b, par, turn):
                    n = [0]

                    def link(ins):
                        n[0] += 1
                        ins.then_inc(f_v, 1)
                        dve.wait_ge(f_v, b * STEPS_V + n[0])

                    dve.wait_ge(f_rows[par], (turn + 1) * NTOK * TOPK * 16)
                    dve.wait_ge(f_ab[par], (turn + 1) * 16)
                    t = b * NTOK
                    for j in range(NTOK):
                        link(nc.vector.tensor_scalar(moe[:, j, :], rows[par][:, 0, j, :], top[:, bass.ds(t + j, 1), 0], None, ALU.mult))
                        link(nc.vector.scalar_tensor_tensor(out=moe[:, j, :], in0=rows[par][:, 1, j, :],
                                                            scalar=top[:, bass.ds(t + j, 1), 1], in1=moe[:, j, :],
                                                            op0=ALU.mult, op1=ALU.add))
                        link(nc.vector.tensor_tensor_reduce(junk[:, :], ab[par][:, j, :], gcw[:, 0, :], 1.0, 0.0,
                                                            ALU.mult, ALU.add, dot[:, 0, j:j + 1]))
                        link(nc.vector.tensor_tensor_reduce(junk[:, :], moe[:, j, :], gcw[:, 1, :], 1.0, 0.0,
                                                            ALU.mult, ALU.add, dot[:, 1, j:j + 1]))
                    nc.vector.scalar_tensor_tensor(out=gl[:, 0, :], in0=dot[:, 0, :], scalar=gcb[:, 0:1],
                                                   in1=dot[:, 1, :], op0=ALU.add, op1=ALU.add).then_inc(f_x, 1)
                    for j in range(NTOK):
                        link(nc.vector.tensor_scalar(u[:, j, :], xs[:, b, j, :], mv1[:, bass.ds(t + j, 1), 0],
                                                     rstd1[:, bass.ds(t + j, 1)], ALU.subtract, ALU.mult))
                    nv = nc.vector
                    link(nv.tensor_tensor(u[:, :, :], u[:, :, :], ab[par][:, :, :], ALU.add))
                    nv.tensor_tensor(moe[:, :, :], moe[:, :, :], ab[par][:, :, :], ALU.subtract).then_inc(f_free, 1)
                    dve.wait_ge(f_e, b + 1)
                    dve.wait_ge(f_free, b + 1)
                    for j in range(NTOK):
                        link(nv.scalar_tensor_tensor(out=u[:, j, :], in0=moe[:, j, :], scalar=gl[:, 1, j:j + 1],
                                                     in1=u[:, j, :], op0=ALU.mult, op1=ALU.add))
                        link(nv.bn_stats(fst[:, j, :], u[:, j, :]))
                        plain(dve)
                        nv.bn_aggr(fmv[:, j, :], fst[:, j, :]).then_inc(f_mv, 1)
                    assert n[0] == STEPS_V
                    dve.wait_ge(f_rs, b + 1)
                    dve.wait_ge(f_out[par], turn * len(RUNS) * 16)
                    for j in range(NTOK):
                        nv.tensor_scalar(o[par][:, j, :], u[:, j, :], fmv[:, j, 0:1], frs[:, j:j + 1],
                                         ALU.subtract, ALU.mult).then_inc(f_first, 1)
                        dve.wait_ge(f_first, b * NTOK + j + 1)
                        nv.tensor_tensor(o[par][:, j, :], o[par][:, j, :], xs[:, b, j, :], ALU.add).then_inc(f_o, 1)

                pairs(dve, batch)


def sandwich_kernel(nc, a):
    B, S, D = a["x"].shape
    with ExitStack() as outer:
        xs = outer.enter_context(nc.sbuf_tensor("xs", [P, B, S // P, D], F32))
        attention(nc, outer, a["x"], xs, a["wqkvT"], a["bqk"], a["bv_rep"], a["ident"], a["qrows"], a["krows"])
        ffn(nc, xs, a, a["out"])


def kernel(**inputs):
    import numpy as np
    import concourse.bacc as bacc
    from concourse.bass_utils import run_bass_kernel_spmd

    at = {k[len("L0_attn_"):]: np.asarray(v) for k, v in inputs.items() if k.startswith("L0_attn_")}
    ff = {k[len("L0_ffn_"):]: np.asarray(v) for k, v in inputs.items() if k.startswith("L0_ffn_")}
    x = at["hidden_states"]
    B, S, D = x.shape

    def rep(v):
        return np.broadcast_to(v, (P,) + v.shape)

    def by_feature(v):
        return v.reshape(-1, P).T

    qrows, krows, ident = constants()
    arrays = {
        "x": x,
        "wqkvT": np.concatenate([at["Wq"].T, at["Wk"].T, at["Wv"].T], 1),
        "bqk": np.stack([by_feature(at["bq"]), by_feature(at["bk"])], 2).reshape(P, 2 * D // P),
        "bv_rep": rep(np.stack([at["bv"], at["bv"]])),
        "ident": ident, "qrows": qrows, "krows": krows,
        "consts": ffn_constants(B * S),
        "wab": np.concatenate([ff["abel_w"], ff["moe_gate_w"]], 1),
        "bias_ab": rep(np.concatenate([ff["abel_b"], ff["moe_gate_b"]])),
        "affine": np.stack([by_feature(ff["ln_gamma"]), by_feature(ff["ln_beta"])], 1),
        "gens": ff["gens"], "gensT": ff["gens"].transpose(0, 2, 1),
        "ew1": ff["ew1"], "eb1": ff["eb1"].reshape(NE, -1, P).transpose(2, 0, 1),
        "ew2T": ff["ew2"].transpose(0, 2, 1), "eb2T": ff["eb2"].T,
        "gcw": rep(ff["gc_w"].reshape(2, D)), "gcb": rep(ff["gc_b"]),
    }
    nc = bacc.Bacc("TRN2", target_bir_lowering=False, num_devices=1)
    given, aps = {}, {}
    for name, v in arrays.items():
        v = np.ascontiguousarray(v)
        given[f"in_{name}"] = v
        aps[name] = nc.dram_tensor(f"in_{name}", v.shape, mybir.dt.from_np(v.dtype), kind="ExternalInput").ap()
    aps["out"] = nc.dram_tensor("out_0", x.shape, F32, kind="ExternalOutput").ap()
    sandwich_kernel(nc, aps)
    r = run_bass_kernel_spmd(nc, [given], core_ids=[0])
    return r.results[0]["out_0"]
```

```python
from contextlib import ExitStack

import concourse.bass as bass
from concourse import mybir

F32 = mybir.dt.float32
BF16 = mybir.dt.bfloat16
I32 = mybir.dt.int32
U32 = mybir.dt.uint32
ALU = mybir.AluOpType
ACT = mybir.ActivationFunctionType
AX_X = mybir.AxisListType.X

P = 128
EPS = 1e-5
HEADS, DH, BLK = 16, 16, 64

ORDER = [1, 2, 0, 7, 3, 4, 5, 6]
MEETS = [[(0, 320)], [(0, 512)], [(64, 448)], [(128, 256), (320, 512)]]
NT = len(MEETS)
CHUNKS = [
    [(1, 0, 0, 512)],
    [(0, 0, 0, 320), (2, 320, 64, 256)],
    [(2, 0, 256, 448), (3, 192, 128, 256), (3, 320, 320, 512)],
]
NCH = len(CHUNKS)
RUNS = [(0, 1, 2), (2, 0, 1), (3, 7, 1), (4, 3, 2), (6, 5, 2)]

Q_PART = [0, 0, 1, 1, 0, 2]
K_PART = [0, 1, 0, 1, 2, 0]
NGRP = len(Q_PART)
MASK_ROW = NGRP * DH
N_MASK = 4
MAX_ROW = MASK_ROW + N_MASK
N_MAX = 2
K_SCORE = MAX_ROW
K_EXP = MAX_ROW + N_MAX
BIG = 1e30
HOLES = [((1, 5), (3,)), ((2, 6), (4,)), ((3,), (1, 5)), ((4,), (2, 6))]

GROUP = 4
NG = HEADS // GROUP
UNITS = HEADS * NCH
QUADS = UNITS // GROUP
NPB = 8
B_FROM = 3


def tile(ap, t):
    return ap[:, t * P:(t + 1) * P]


def attention(nc, outer, x, xs, wqkvT, bqk, bv_rep, ident, qrows, krows):
    B, S, D = x.shape
    NTOK = S // P
    KC = D // P
    assert D == HEADS * DH and S == 8 * BLK
    ctx = ExitStack()
    with ctx:
        def sb(name, shape, dt=F32):
            return ctx.enter_context(nc.sbuf_tensor(name, shape, dt))

        def ps(name, shape, dt=F32):
            return ctx.enter_context(nc.psum_tensor(name, shape, dt))

        def sem(name):
            return outer.enter_context(nc.semaphore(name))

        wqkv = sb("wqkv", [P, KC, 3 * D])
        bqk_sb = sb("bqk_sb", [P, 4])
        bv_sb = sb("bv_sb", [P, 2, D])
        ident_sb = sb("ident_sb", [P, P])
        neg_half = sb("neg_half", [P, NTOK])
        stat = sb("stat", [P, NTOK, 6])
        mv = sb("mv", [P, NTOK, 2])
        veps = sb("veps", [P, NTOK])
        rstd = sb("rstd", [P, NTOK])
        xn = sb("xn", [P, NTOK, D])
        xnT = sb("xnT", [P, KC, S])
        split = sb("split", [P, 4, 3, S], BF16)
        resid = sb("resid", [P, 2, S])
        rows_sb = resid
        qst = [sb(f"qst{i}", [P, HEADS, S], BF16) for i in range(2)]
        kst = [sb(f"kst{i}", [P, HEADS, S], BF16) for i in range(2)]
        vaug = [sb(f"vaug{i}", [P, NT, HEADS, 32]) for i in range(2)]
        mx = sb("mx", [P, NT * HEADS])
        mrow = sb("mrow", [NT * HEADS, N_MAX, P], BF16)
        pexp = sb("pexp", [P, NPB, S])
        ctxT = sb("ctxT", [P, NG, S])
        rden = sb("rden", [P, 2, HEADS])
        ctxn = sb("ctxn", [P, NTOK, D])
        cstat = sb("cstat", [P, NTOK, 6])
        cmv = sb("cmv", [P, NTOK, 2])
        cveps = sb("cveps", [P, NTOK])
        crstd = sb("crstd", [P, NTOK])
        shift = sb("x_shift", [P, NTOK])
        cshift = sb("ctx_shift", [P, NTOK])

        work = [ps(f"work{i}", [P, S]) for i in range(4)]
        scT = [ps(f"scT{i}", [P, S]) for i in range(2)]
        pv = ps("pv", [P, S])
        turn = ps("turn", [P, S])

        spill = nc.dram_tensor("split_spill", [2, 4, P, 3, S], BF16, kind="Internal").ap()

        s_const = sem("s_const")
        s_rows = sem("s_rows")
        s_xin = [sem(f"s_xin{i}") for i in range(2)]
        s_stat = sem("s_stat")
        s_veps = sem("s_veps")
        s_rstd = sem("s_rstd")
        s_shift = sem("s_shift")
        s_cshift = sem("s_cshift")
        s_xn = sem("s_xn")
        s_bn = sem("s_bn")
        w_full = [sem(f"w_full{i}") for i in range(4)]
        w_free = [sem(f"w_free{i}") for i in range(4)]
        s_part1 = sem("s_part1")
        s_part2 = sem("s_part2")
        s_split = sem("s_split")
        s_spill = [sem(f"s_spill{i}") for i in range(2)]
        s_stack = [sem(f"s_stack{i}") for i in range(2)]
        s_m1 = sem("s_m1")
        s_mrow = sem("s_mrow")
        s_sc = sem("s_sc")
        s_exp = sem("s_exp")
        s_pv = sem("s_pv")
        s_ctxT = sem("s_ctxT")
        s_turn = sem("s_turn")
        s_rden = sem("s_rden")
        s_ctxn = sem("s_ctxn")
        s_cbn = sem("s_cbn")
        s_cstat = sem("s_cstat")
        s_cveps = sem("s_cveps")
        s_crstd = sem("s_crstd")
        s_xt = sem("s_xt")
        s_xnT = sem("s_xnT")
        s_cln = sem("s_cln")
        s_x1 = sem("s_x1")
        s_vpad = sem("s_vpad")
        N_CONST = 6

        BEFORE_MAX = [1, 1, 2, 2]
        W_USES = [BEFORE_MAX[w] + HEADS + (w == 0) for w in range(4)]
        NORM_CTX, NORM_X = 5, 6
        TURN_XN = [8, 10]
        block = ctx.enter_context(nc.Block())

        def wait(eng, s, value):
            if not isinstance(value, int) or value > 0:
                eng.wait_ge(s, value)

        def plain(eng):
            eng.nop(nofuse=True)

        def steps(eng, step):
            for s in range(4):
                step(s, s % 2)
            with eng.Fori(2, B // 2 - 1) as i:
                step(2 * i, 0)
                step(2 * i + 1, 1)
            for s in range(B - 2, B + 2):
                step(s, s % 2)

        def nth_load(b, par):
            return (b + 2 - par) // 2

        def doing(s):
            if not isinstance(s, int):
                return True, True, True
            return s < B, 1 <= s <= B, 2 <= s

        def load_x(sp, b, par):
            for pos, blk, n in RUNS:
                lo = pos % 2 * BLK
                sp.dma_start(xs[lo:lo + n * BLK, b, pos // 2, :], x[b, blk * BLK:(blk + n) * BLK, :])\
                  .then_inc(s_xin[par], 16)

        @block.sync
        def _(sp):
            sp.dma_start(ident_sb[:, :], ident).then_inc(s_const, 16)
            sp.dma_start(wqkv[:, :, :], wqkvT.rearrange("(k p) o -> p k o", p=P)).then_inc(s_const, 16)
            sp.dma_start(bqk_sb[:, :], bqk).then_inc(s_const, 16)
            sp.dma_start(bv_sb[:, :, :], bv_rep).then_inc(s_const, 16)
            sp.dma_start(rows_sb[MASK_ROW:K_EXP, 0, :], qrows).then_inc(s_const, 16)
            sp.dma_start(rows_sb[MASK_ROW:K_EXP, 1, :], krows).then_inc(s_const, 16)
            load_x(sp, 0, 0)
            load_x(sp, 1, 1)

            def step(s, par):
                project, attend, finish = doing(s)
                if not project:
                    return
                b = s
                if not isinstance(b, int) or b + 2 < B:
                    sp.wait_ge(s_bn, (b + 1) * NTOK)
                    load_x(sp, b + 2, par)
                wait(sp, s_sc, (b - 1) * UNITS)
                plain(sp)
                if isinstance(b, int) and b < 2:
                    sp.wait_ge(s_rows, 4)
                for half in range(2):
                    for m in range(2 * half, 2 * half + 2):
                        sp.wait_ge(s_split, b * 4 + m + 1)
                        sp.dma_start(spill[par, m], split[:, m, :, :]).then_inc(s_spill[half], 16)
                    sp.wait_ge(s_spill[half], b * 32 + 32)
                    for st, m, parts in ((qst, 2 * half, Q_PART), (kst, 2 * half + 1, K_PART)):
                        for g, part in enumerate(parts):
                            src = spill[par, m].rearrange("(h d) s c -> d h s c", d=DH)[:, :, part, :]
                            sp.dma_start(st[par][g * DH:(g + 1) * DH, 8 * half:8 * half + 8, :], src)\
                              .then_inc(s_stack[half], 16)
                sp.wait_ge(w_free[0], b * W_USES[0] + W_USES[0])
                for t in range(NT):
                    for part in range(N_MAX):
                        r = MAX_ROW + part
                        sp.dma_start(qst[par][r:r + 1, :, t * P:(t + 1) * P],
                                     mrow[t * HEADS:(t + 1) * HEADS, part, :]).then_inc(s_mrow, 16)

            steps(sp, step)

        @block.tensor
        def _(pe):
            pe.wait_ge(s_const, N_CONST * 16)

            def use(w, b, n):
                wait(pe, w_free[w], b * W_USES[w] + n)

            def turn_xn(b, k):
                if k == 0:
                    wait(pe, s_ctxn, (b - 2) * NTOK)
                wait(pe, s_xnT, b * KC + k)
                for j in range(NTOK):
                    pe.wait_ge(s_xn, b * NTOK + j + 1)
                    ins = nc.tensor.transpose(turn[:, j * P:(j + 1) * P], xn[:, j, k * P:(k + 1) * P],
                                              ident_sb[:, :])
                ins.then_inc(s_xt, 1)

            def project(b, m):
                if m == 0:
                    pe.wait_ge(s_xnT, (b + 1) * KC)
                w = (2 + m) % 4
                col = (m % 2) * D + (m // 2) * P
                use(w, b, 0)
                for k in range(KC):
                    ins = nc.tensor.matmul(work[w][:, :], wqkv[:, k, col:col + P], xnT[:, k, :],
                                           start=(k == 0), stop=(k == KC - 1))
                ins.then_inc(w_full[w], 1)

            def project_v(b, t):
                w, n = 2 + t // 2, t % 2
                if n == 0:
                    use(w, b, 1)
                for k in range(KC):
                    ins = nc.tensor.matmul(work[w][:, n * D:(n + 1) * D], tile(xnT[:, k, :], t),
                                           wqkv[:, k, 2 * D:3 * D], start=(k == 0), stop=(k == KC - 1))
                if n == 1:
                    ins.then_inc(w_full[w], 1)

            def max_unit(b, par, h, t):
                if t == 0 and h % 8 == 0:
                    pe.wait_ge(s_stack[h // 8], (b + 1) * 2 * NGRP * 16)
                use(t, b, BEFORE_MAX[t] + h)
                at = 0
                for lo, hi in MEETS[t]:
                    ins = nc.tensor.matmul(work[t][:, at:at + hi - lo], tile(qst[par][0:K_SCORE, h, :], t),
                                           kst[par][0:K_SCORE, h, lo:hi], start=True, stop=True)
                    at += hi - lo
                ins.then_inc(w_full[t], 1)

            def turn_max(b):
                for t in range(NT):
                    pe.wait_ge(w_free[t], b * W_USES[t] + BEFORE_MAX[t] + HEADS)
                plain(pe)
                nc.tensor.transpose(work[0][0:NT * HEADS, 0:P], mx[:, :], ident_sb[:, :]).then_inc(w_full[0], 1)

            def score_unit(b, par, q, n):
                h, c = q // NCH * GROUP + n, q % NCH
                u = b * UNITS + q * GROUP + n
                if q == 0 and n == 0:
                    pe.wait_ge(s_mrow, (b + 1) * NT * N_MAX * 16)
                wait(pe, s_exp, u - 1)
                for t, at, lo, hi in CHUNKS[c]:
                    ins = nc.tensor.matmul(scT[n % 2][:, at:at + hi - lo],
                                           tile(kst[par][0:K_EXP, h, :], t),
                                           qst[par][0:K_EXP, h, lo:hi], start=True, stop=True)
                ins.then_inc(s_sc, 1)

            def pv_half(b, par, q, half):
                g, c = q // NCH, q % NCH
                if half == 0:
                    pe.wait_ge(s_exp, b * UNITS + (q + 1) * GROUP)
                    if q == 0:
                        for w in (2, 3):
                            pe.wait_ge(w_free[w], b * W_USES[w] + 2)
                    if c == 0:
                        wait(pe, s_ctxT, b * NG + g)
                products = [(chunk, n) for chunk in CHUNKS[c] for n in range(GROUP)]
                middle = len(products) // 2
                for (t, at, lo, hi), n in products[half * middle:(half + 1) * middle]:
                    h = g * GROUP + n
                    last = c == NCH - 1 and (t, at, lo, hi) == CHUNKS[c][-1]
                    ins = nc.tensor.matmul(pv[32 * n:32 * n + 32, lo:hi], vaug[par][:, t, h, :],
                                           pexp[:, (q * GROUP + n) % NPB, at:at + hi - lo],
                                           start=(c == 0), stop=last, skip_group_check=True)
                if half == 1:
                    ins.then_inc(s_pv, 1)

            def turn_ctx(b, j):
                if j == 0:
                    pe.wait_ge(s_ctxT, (b + 1) * NG)
                    if isinstance(b, int):
                        pe.wait_ge(s_xnT, min(b + 3, B) * KC)
                    else:
                        pe.wait_ge(s_xnT, (b + 3) * KC)
                wait(pe, s_ctxn, b * NTOK + j)
                for g in range(NG):
                    ins = nc.tensor.transpose(turn[:, g * P:(g + 1) * P], ctxT[:, g, j * P:(j + 1) * P],
                                              ident_sb[:, :])
                ins.then_inc(s_turn, 1)

            def step(s, par):
                proj, attend, finish = doing(s)
                for m in range(4):
                    if proj:
                        project(s, m)
                    if finish and m % 2:
                        turn_ctx(s - 2, m // 2)
                units = [(h, t) for h in range(HEADS) for t in range(NT)] if proj else []
                for q in range(QUADS):
                    if q in TURN_XN and (not isinstance(s, int) or s + 1 < B):
                        turn_xn(s + 1, TURN_XN.index(q))
                    fill = units[max(q - B_FROM, 0) * len(units) // (QUADS - B_FROM):
                                 max(q - B_FROM + 1, 0) * len(units) // (QUADS - B_FROM)]
                    third = -(-len(fill) // 3)
                    for n in range(GROUP):
                        if attend:
                            score_unit(s - 1, 1 - par, q, n)
                        if n in (1, 2) and proj and q < NT // 2:
                            project_v(s, 2 * q + n - 1)
                        if n == 2 and finish and q in (1, 2):
                            turn_ctx(s - 2, q + 1)
                        if n > 0:
                            for h, t in fill[(n - 1) * third:n * third]:
                                max_unit(s, par, h, t)
                        if attend and q > 0 and n % 2:
                            pv_half(s - 1, 1 - par, q - 1, n // 2)
                if proj:
                    turn_max(s)
                if attend:
                    for half in range(2):
                        pv_half(s - 1, 1 - par, QUADS - 1, half)

            for k in range(KC):
                turn_xn(0, k)
            steps(pe, step)

        @block.scalar
        def _(act):
            act.wait_ge(s_const, N_CONST * 16)

            def evac_xnT(b, k):
                act.wait_ge(s_xt, b * KC + k + 1)
                nc.scalar.copy(xnT[:, k, :], turn[:, :]).then_inc(s_xnT, 1)

            def first_part(b):
                for m in range(4):
                    w = (2 + m) % 4
                    act.wait_ge(w_full[w], b * W_USES[w] + 1)
                    if m % 2 == 0:
                        wait(act, s_spill[m // 2], b * 32)
                    nc.scalar.activation(split[:, m, 0, :], work[w][:, :], ACT.Identity,
                                         bias=bqk_sb[:, m:m + 1]).then_inc(s_part1, 1)

            def first_max(b):
                act.wait_ge(w_full[0], b * W_USES[0] + W_USES[0])
                wait(act, s_mrow, b * NT * N_MAX * 16)
                nc.scalar.copy(mrow[:, 0, :], work[0][0:NT * HEADS, 0:P]).then_inc(s_m1, 1)

            def norm_x(b, j):
                if j == 0:
                    act.wait_ge(s_shift, b + 1)
                    plain(act)
                nc.scalar.activation(xn[:, j, :], xs[:, b, j, :], ACT.Identity, scale=rstd[:, j:j + 1],
                                     bias=shift[:, j:j + 1]).then_inc(s_xn, 1)

            def norm_ctx(b, j):
                if j == 0:
                    act.wait_ge(s_cshift, b + 1)
                nc.scalar.activation(ctxn[:, j, :], ctxn[:, j, :], ACT.Identity, scale=crstd[:, j:j + 1],
                                     bias=cshift[:, j:j + 1]).then_inc(s_cln, 1)

            def exps(b, q, n):
                u = b * UNITS + q * GROUP + n
                act.wait_ge(s_sc, u + 1)
                if n == 0:
                    wait(act, s_pv, b * QUADS + q - NPB // GROUP + 1)
                nc.scalar.activation(pexp[:, (q * GROUP + n) % NPB, :], scT[n % 2][:, :], ACT.Exp,
                                     scale=DH ** -0.5).then_inc(s_exp, 1)

            def evac_ctx(b, g):
                act.wait_ge(s_pv, b * QUADS + (g + 1) * NCH)
                if g == 0:
                    wait(act, s_turn, b * NTOK)
                nc.scalar.copy(ctxT[:, g, :], pv[:, :]).then_inc(s_ctxT, 1)

            def step(s, par):
                proj, attend, finish = doing(s)
                if proj:
                    first_part(s)
                for q in range(QUADS):
                    for n in range(GROUP):
                        if attend:
                            exps(s - 1, q, n)
                        if q == NORM_CTX and finish:
                            norm_ctx(s - 2, n)
                        if q == NORM_X and (not isinstance(s, int) or s + 1 < B):
                            norm_x(s + 1, n)
                    if attend and q > 0 and q % NCH == 0:
                        evac_ctx(s - 1, q // NCH - 1)
                    if q in TURN_XN and (not isinstance(s, int) or s + 1 < B):
                        evac_xnT(s + 1, TURN_XN.index(q))
                if proj:
                    first_max(s)
                if attend:
                    evac_ctx(s - 1, NG - 1)

            for j in range(NTOK):
                norm_x(0, j)
            for k in range(KC):
                evac_xnT(0, k)
            steps(act, step)

        @block.vector
        def _(dve):
            nc.vector.memset(neg_half[:, :], -0.5).then_inc(s_rows, 1)
            for i in range(2):
                nc.vector.memset(vaug[i][:, :, :, DH:32], 0.0).then_inc(s_vpad, 1)
            dve.wait_ge(s_vpad, 2)
            for i in range(2):
                nc.vector.memset(vaug[i][:, :, :, DH:DH + 1], 1.0).then_inc(s_vpad, 1)
            dve.wait_ge(s_const, N_CONST * 16)
            for i in range(2):
                for st, r in ((qst, 0), (kst, 1)):
                    src = rows_sb[MASK_ROW:K_EXP, r, :].rearrange("p (o c) -> p o c", o=1)
                    nc.vector.tensor_copy(st[i][MASK_ROW:K_EXP, :, :],
                                          src.broadcast_to([K_EXP - MASK_ROW, HEADS, S])).then_inc(s_rows, 1)

            def stats(b):
                for j in range(NTOK):
                    nc.vector.bn_stats(stat[:, j, :], xs[:, b, j, :]).then_inc(s_bn, 1)
                dve.wait_ge(s_bn, (b + 1) * NTOK)
                plain(dve)
                for j in range(NTOK):
                    nc.vector.bn_aggr(mv[:, j, :], stat[:, j, :]).then_inc(s_stat, 1)

            def negated(b, ready, mean, inv, dst, dst_sem):
                dve.wait_ge(ready, b + 1)
                nc.vector.scalar_tensor_tensor(out=dst[:, :], in0=mean, scalar=-1.0, in1=inv[:, :],
                                               op0=ALU.mult, op1=ALU.mult).then_inc(dst_sem, 1)

            def parts(b, m):
                w = (2 + m) % 4
                dve.wait_ge(s_part1, b * 4 + m + 1)
                nc.vector.scalar_tensor_tensor(out=resid[:, m % 2, :], in0=work[w][:, :],
                                               scalar=bqk_sb[:, m:m + 1], in1=split[:, m, 0, :],
                                               op0=ALU.add, op1=ALU.subtract).then_inc(w_free[w], 1)
                dve.wait_ge(w_free[w], b * W_USES[w] + 1)
                nc.vector.tensor_copy(split[:, m, 1, :], resid[:, m % 2, :]).then_inc(s_part2, 1)
                dve.wait_ge(s_part2, b * 4 + m + 1)
                nc.vector.tensor_tensor(split[:, m, 2, :], resid[:, m % 2, :], split[:, m, 1, :],
                                        ALU.subtract).then_inc(s_split, 1)

            def values(b, par, n):
                dve.wait_ge(w_full[2 + n], b * W_USES[2 + n] + 2)
                nc.vector.tensor_tensor(
                    vaug[par][:, 2 * n:2 * n + 2, :, 0:DH],
                    work[2 + n][:, :].rearrange("p (t h d) -> p t h d", t=2, d=DH),
                    bv_sb[:, :, :].rearrange("p t (h d) -> p t h d", d=DH), ALU.add)\
                  .then_inc(w_free[2 + n], 1)

            def maximum(b, h, t):
                dve.wait_ge(w_full[t], b * W_USES[t] + BEFORE_MAX[t] + 1 + h)
                n = sum(hi - lo for lo, hi in MEETS[t])
                c = t * HEADS + h
                nc.vector.reduce_max(mx[:, c:c + 1], work[t][:, 0:n], AX_X).then_inc(w_free[t], 1)

            def second_max(b):
                dve.wait_ge(s_m1, b + 1)
                nc.vector.tensor_tensor(mrow[:, 1, :], work[0][0:NT * HEADS, 0:P], mrow[:, 0, :],
                                        ALU.subtract).then_inc(w_free[0], 1)

            def finish_a(b, j):
                dve.wait_ge(s_turn, b * NTOK + j + 1)
                tv = turn[:, :].rearrange("p (h e) -> p h e", e=32)
                nc.vector.reciprocal(rden[:, j % 2, :], tv[:, :, DH]).then_inc(s_rden, 1)
                dve.wait_ge(s_rden, b * NTOK + j + 1)
                if j == 0:
                    wait(dve, s_x1, b * NTOK)
                inv = rden[:, j % 2, :].rearrange("p (h o) -> p h o", o=1).broadcast_to([P, HEADS, DH])
                nc.vector.tensor_tensor(ctxn[:, j, :].rearrange("p (h d) -> p h d", d=DH),
                                        tv[:, :, 0:DH], inv, ALU.mult).then_inc(s_ctxn, 1)
                dve.wait_ge(s_ctxn, b * NTOK + j + 1)
                nc.vector.bn_stats(cstat[:, j, :], ctxn[:, j, :]).then_inc(s_cbn, 1)
                dve.wait_ge(s_cbn, b * NTOK + j + 1)
                plain(dve)
                nc.vector.bn_aggr(cmv[:, j, :], cstat[:, j, :]).then_inc(s_cstat, 1)

            def step(s, par):
                proj, attend, finish = doing(s)
                if isinstance(s, int) and s == 0:
                    dve.wait_ge(s_xin[0], len(RUNS) * 16)
                    stats(0)
                    negated(0, s_rstd, mv[:, :, 0], rstd, shift, s_shift)
                for m in range(4):
                    if proj:
                        parts(s, m)
                    if finish and m % 2:
                        finish_a(s - 2, m // 2)
                if finish:
                    finish_a(s - 2, 2)
                more = not isinstance(s, int) or s + 1 < B
                if more:
                    dve.wait_ge(s_xin[1 - par], nth_load(s + 1, 1 - par) * len(RUNS) * 16)
                    stats(s + 1)
                if finish:
                    finish_a(s - 2, 3)
                if proj:
                    for n in range(2):
                        values(s, par, n)
                if finish:
                    negated(s - 2, s_crstd, cmv[:, :, 0], crstd, cshift, s_cshift)
                units = [(h, t) for h in range(HEADS) for t in range(NT)] if proj else []
                if more:
                    negated(s + 1, s_rstd, mv[:, :, 0], rstd, shift, s_shift)
                for h, t in units:
                    maximum(s, h, t)
                if proj:
                    second_max(s)

            steps(dve, step)

        @block.gpsimd
        def _(pool):
            pool.wait_ge(s_rows, 1)

            def inverse(n, ready, per, var, mid, mid_sem, dst, dst_sem):
                pool.wait_ge(ready, per * n + per)
                plain(pool)
                nc.gpsimd.tensor_scalar(mid[:, :], var, EPS, None, ALU.add).then_inc(mid_sem, 1)
                pool.wait_ge(mid_sem, n + 1)
                nc.gpsimd.tensor_tensor(dst[:, :], mid[:, :], neg_half[:, :], ALU.pow).then_inc(dst_sem, 1)

            def ln1(b):
                inverse(b, s_stat, NTOK, mv[:, :, 1], veps, s_veps, rstd, s_rstd)

            def step(s, par):
                proj, attend, finish = doing(s)
                if isinstance(s, int) and s == 0:
                    ln1(0)
                if not isinstance(s, int) or s + 1 < B:
                    ln1(s + 1)
                if finish:
                    b = s - 2
                    inverse(b, s_cstat, NTOK, cmv[:, :, 1], cveps, s_cveps, crstd, s_crstd)
                    for j in range(NTOK):
                        pool.wait_ge(s_cln, b * NTOK + j + 1)
                        nc.gpsimd.tensor_tensor(xs[:, b, j, :], xs[:, b, j, :], ctxn[:, j, :], ALU.add)\
                          .then_inc(s_x1, 1)

            steps(pool, step)


def constants():
    import numpy as np
    q = np.zeros((N_MASK + N_MAX, 8 * BLK), np.float32)
    k = np.zeros((N_MASK + N_MAX, 8 * BLK), np.float32)
    for r, (left, right) in enumerate(HOLES):
        for pos, blk in enumerate(ORDER):
            cols = slice(pos * BLK, (pos + 1) * BLK)
            if blk in left:
                q[r, cols] = 1.0
            if blk in right:
                k[r, cols] = -BIG
    k[N_MASK:] = -1.0
    return q, k, np.eye(P, dtype=np.float32)


NE = 8
TOPK = 2
RT = 256
NROT = 3

def routed_sizes(tokens):
    region = tokens + RT
    tiles = (TOPK * tokens + NE * (RT - 1)) // RT
    return region, tiles + tiles % 2


def ffn_constants(tokens):
    import numpy as np
    region, tiles = routed_sizes(tokens)
    before = np.triu(np.ones((P, P), np.float32), 1)
    wide = np.concatenate([np.arange(NE), np.arange(NE) * region, np.arange(tiles)]).astype(np.float32)
    return np.concatenate([np.eye(P, dtype=np.float32), before, np.broadcast_to(wide, (P, wide.size))], 1)


def ffn(nc, xs, w, out):
    _, B, NTOK, D = xs.shape
    KC = D // P
    TILES = B * NTOK
    TOKENS = TILES * P
    F = w["ew1"].shape[2]
    FC = F // P
    REGION, RTILES = routed_sizes(TOKENS)
    RB = RT // P
    HALVINGS = B // 2

    ctx = ExitStack()
    with ctx:
        def sb(name, shape, dt=F32, where=ctx):
            return where.enter_context(nc.sbuf_tensor(name, shape, dt))

        def sem(name):
            return ctx.enter_context(nc.semaphore(name))

        def wait(eng, s, value):
            if not isinstance(value, int) or value > 0:
                eng.wait_ge(s, value)

        def plain(eng):
            eng.nop(nofuse=True)

        z_rows = nc.dram_tensor("z_rows", [NE * REGION, D], F32, kind="Internal").ap()
        y_rows = nc.dram_tensor("y_rows", [RTILES * RT, D], F32, kind="Internal").ap()
        abel_rows = nc.dram_tensor("abel_rows", [TILES * P, D], F32, kind="Internal").ap()
        eb2_spill = nc.dram_tensor("eb2_spill", [NE, D], F32, kind="Internal").ap()

        cst = sb("cst", [P, 2 * P + 2 * NE + RTILES])
        ident, numbers = cst[:, 0:P], cst[:, 2 * P:2 * P + NE]
        first_row, tile_no = cst[:, 2 * P + NE:2 * P + 2 * NE], cst[:, 2 * P + 2 * NE:]
        affine = sb("affine", [P, 2, KC])
        mv1 = sb("mv1", [P, TILES, 2])
        rstd1 = sb("rstd1", [P, TILES])
        region_row = sb("region_row", [P, TILES, TOPK])
        result_row = sb("result_row", [P, TILES, TOPK], U32)
        top = sb("top", [P, TILES, TOPK])
        neg_half = sb("neg_half4", [P, NTOK])
        table = sb("table", [P, 2, RTILES], I32)
        tail = sb("tail", [P, NE], I32)

        weights_ctx = ctx.enter_context(ExitStack())
        w1 = sb("w1", [P, NE, KC, F], F32, weights_ctx)
        w2 = sb("w2", [P, NE, FC, D], F32, weights_ctx)
        b1 = sb("b1", [P, NE, FC], F32, weights_ctx)
        b2 = sb("b2", [P, NE, D], F32, weights_ctx)

        g_load = sem("g_load")
        g_weights = sem("g_weights")
        g_table = sem("g_table")

        gate_ctx = ExitStack()
        with gate_ctx:
            def gsb(name, shape, dt=F32):
                return sb(name, shape, dt, gate_ctx)

            wab = gsb("wab", [P, KC, D + NE])
            bias_ab = gsb("bias_ab", [P, D + NE])
            before = gsb("before", [P, P], BF16)
            ones = gsb("ones", [P, P], BF16)
            z = [gsb(f"z{i}", [P, NTOK, D]) for i in range(4)]
            mv0 = gsb("mv0", [P, NTOK, 2])
            st1 = gsb("st1", [P, NTOK, 6])
            ve = gsb("ve", [P, 2, NTOK])
            rs = gsb("rs", [P, 2, NTOK])
            neg_halves = gsb("neg_halves", [P, 2, NTOK])
            zT = gsb("zT", [P, KC, NTOK * P])
            pre = gsb("pre", [P, NTOK, D])
            logit = gsb("logit", [P, NTOK, NE])
            best = gsb("best", [P, NTOK, NE])
            best_i = gsb("best_i", [P, NTOK, NE], U32)
            best_f = gsb("best_f", [P, TOPK, NTOK])
            hot = gsb("hot", [P, TOPK, NTOK, NE])
            chosen = gsb("chosen", [P, NTOK, NE], BF16)
            batch_sum = gsb("batch_sum", [P, NE])
            carry = [gsb(f"carry{i}", [P, NE], BF16) for i in range(2)]
            place = gsb("place", [P, NTOK, NE])
            pick = gsb("pick", [P, TOPK, NTOK, NE])
            dest_f = gsb("dest_f", [P, TOPK, NTOK])
            to_row = [gsb(f"to_row{i}", [P, NTOK, TOPK], U32) for i in range(4)]
            gA = gsb("gA", [P, NROT, KC, D])
            gAT = gsb("gAT", [P, NROT, KC, D])
            gE = gsb("gE", [P, NROT, KC, D])
            gET = gsb("gET", [P, NROT, KC, D])
            prod = gAT
            w2T = [gsb(f"w2T{i}", [P, KC, F]) for i in range(2)]
            eb2T = gsb("eb2T", [P, KC, NE])
            eb2_out = gsb("eb2_out", [NE, D])
            tb = gsb("tb", [P, 5, RTILES])
            cnt = gsb("cnt", [P, 6, NE])
            cnt_i = gsb("cnt_i", [P, 2, NE], I32)
            zero = gsb("zero", [P, RB, D])
            shift = gsb("shift", [P, 2, TILES * TOPK])

            def bank(name):
                return gate_ctx.enter_context(nc.psum_tensor(name, [P, 512], F32))

            zt_ps = [bank(f"zt_ps{k}") for k in range(KC)]
            ab_ps = [bank(f"ab_ps{k}") for k in range(2)]
            lg_ps = bank("lg_ps")
            LG, PL = lg_ps[:, 0:NTOK * NE], lg_ps[:, 64:64 + NTOK * NE]
            rot_ps = [bank(f"rot_ps{k}") for k in range(NROT)]

            g_st = sem("g_st")
            g_mv = sem("g_mv")
            g_mv1 = sem("g_mv1")
            g_ve = sem("g_ve")
            g_rs = sem("g_rs")
            g_z = sem("g_z")
            g_scat = [sem(f"g_scat{i}") for i in range(4)]
            g_zt = sem("g_zt")
            g_ztc = sem("g_ztc")
            g_ab = sem("g_ab")
            g_lg = sem("g_lg")
            g_pre = sem("g_pre")
            g_log = sem("g_log")
            g_abel = sem("g_abel")
            g_abst = sem("g_abst")
            g_best = sem("g_best")
            g_bi = sem("g_bi")
            g_bf = sem("g_bf")
            g_hot = sem("g_hot")
            g_chosen = sem("g_chosen")
            g_bsum = sem("g_bsum")
            g_carry = sem("g_carry")
            g_pl = sem("g_pl")
            g_place = sem("g_place")
            g_pick = sem("g_pick")
            g_df = sem("g_df")
            g_dest = sem("g_dest")
            g_top = sem("g_top")
            g_kept = sem("g_kept")
            g_init = sem("g_init")
            r_full = [sem(f"r_full{i}") for i in range(NROT)]
            r_free = [sem(f"r_free{i}") for i in range(NROT)]
            r_load = sem("r_load")
            r_v = sem("r_v")
            r_w2 = [sem(f"r_w2{i}") for i in range(2)]
            r_eb = sem("r_eb")
            g_tail = sem("g_tail")
            g_exp = sem("g_exp")
            g_t = sem("g_t")

            block = gate_ctx.enter_context(nc.Block())

            def steps(eng, step):
                for s in range(4):
                    step(s, s % 4, s // 2)
                with eng.Fori(1, B // 4 - 1) as i:
                    for n in range(4):
                        step(4 * i + n, n, 2 * i + n // 2)
                for s in range(B - 4, B + 1):
                    step(s, s % 4, s // 2)

            def has(s, batch):
                return not isinstance(s, int) or 0 <= s + batch < B

            SERIES = [6, 30, 120, 360, 720]
            PREP = len(SERIES) + 1
            R_SERIES = 3
            R_PLUS = R_SERIES + 4
            T_DIFF = 1

            def ROT_END(i):
                return PREP + 2 * HALVINGS + (3 if i == 0 else 0)


            @block.sync
            def _(sp):
                sp.dma_start(cst[:, :], w["consts"]).then_inc(g_load, 16)
                sp.dma_start(wab[:, :, :], w["wab"].rearrange("(k p) n -> p k n", p=P)).then_inc(g_load, 16)
                sp.dma_start(bias_ab[:, :], w["bias_ab"]).then_inc(g_load, 16)
                sp.dma_start(affine[:, :, :], w["affine"]).then_inc(g_load, 16)
                for i in range(NROT):
                    sp.dma_start(gA[:, i, :, :], w["gens"][i].rearrange("(k p) n -> p k n", p=P)).then_inc(r_load, 16)
                    sp.dma_start(gAT[:, i, :, :], w["gensT"][i].rearrange("(k p) n -> p k n", p=P)).then_inc(r_load, 16)
                sp.dma_start(eb2T[:, :, :], w["eb2T"].rearrange("(k p) e -> p k e", p=P)).then_inc(r_load, 16)
                sp.dma_start(b1[:, :, :], w["eb1"]).then_inc(g_weights, 16)
                for e in range(2):
                    sp.dma_start(w2T[e][:, :, :], w["ew2T"][e].rearrange("(k p) f -> p k f", p=P)).then_inc(r_w2[e], 16)
                for e in range(NE):
                    sp.dma_start(w1[:, e, :, :], w["ew1"][e].rearrange("(k p) f -> p k f", p=P)).then_inc(g_weights, 16)

                def step(s, ph, pair):
                    if has(s, -1):
                        b = s - 1
                        sp.wait_ge(g_abel, b + 1)
                        dst = abel_rows.rearrange("(b j p) d -> b p j d", j=NTOK, p=P)
                        sp.dma_start(dst[b], pre[:, :, :]).then_inc(g_abst, 16)

                steps(sp, step)
                for e in range(2, NE):
                    sp.wait_ge(r_full[e % 2], ROT_END(e % 2) + (e // 2) * FC // 2)
                    sp.dma_start(w2T[e % 2][:, :, :], w["ew2T"][e].rearrange("(k p) f -> p k f", p=P))\
                      .then_inc(r_w2[e % 2], 16)
                sp.wait_ge(r_eb, 1)
                sp.dma_start(eb2_spill, eb2_out[:, :]).then_inc(g_tail, 16)
                sp.wait_ge(g_tail, 16)
                sp.dma_start(b2[:, :, :], eb2_spill.rearrange("(o e) d -> o e d", o=1).broadcast_to([P, NE, D])).then_inc(g_tail, 16)
                sp.wait_ge(g_table, 1)
                for e in range(NE):
                    row = sp.value_load(tail[0:1, e:e + 1], min_val=e * REGION, max_val=e * REGION + TOKENS)
                    sp.dma_start(z_rows[bass.ds(row, RT), :].rearrange("(r p) d -> p r d", p=P), zero[:, :, :])\
                      .then_inc(g_tail, 16)
                sp.wait_ge(g_tail, 16 * (2 + NE))
                sp.wait_ge(g_abst, 16 * B)
                sp.wait_ge(g_weights, 16 * (1 + NE))

            @block.tensor
            def _(pe):
                pe.wait_ge(g_load, 4 * 16)
                pe.wait_ge(g_init, 7)

                def product(i, n, lhsT, rhs):
                    pe.wait_ge(r_free[i], n)
                    for m in range(KC):
                        for k in range(KC):
                            ins = nc.tensor.matmul(rot_ps[i][:, m * D:(m + 1) * D], lhsT[:, k, m * P:(m + 1) * P],
                                                   rhs[:, k, :], start=(k == 0), stop=(k == KC - 1))
                    ins.then_inc(r_full[i], 1)

                def turned(i, n, src):
                    pe.wait_ge(r_free[i], n)
                    for m in range(KC):
                        for k in range(KC):
                            ins = nc.tensor.transpose(rot_ps[i][:, m * D + k * P:m * D + (k + 1) * P],
                                                      src[:, k, m * P:(m + 1) * P], ident)
                    ins.then_inc(r_full[i], 1)

                pe.wait_ge(r_v, 2)
                for n in range(len(SERIES)):
                    for i in range(NROT):
                        product(i, n, gAT[:, i], (gE if n else gA)[:, i])
                pe.wait_ge(r_v, R_SERIES)
                for i in range(NROT):
                    turned(i, len(SERIES), gE[:, i])

                def gate(b):
                    for k in range(KC):
                        pe.wait_ge(g_ztc, b * KC + k)
                        for j in range(NTOK):
                            pe.wait_ge(g_z, b * NTOK + j + 1)
                            ins = nc.tensor.transpose(zt_ps[k][:, j * P:(j + 1) * P], z_of(b)[:, j, k * P:(k + 1) * P], ident)
                        ins.then_inc(g_zt, 1)

                def dense(b):
                    pe.wait_ge(g_ztc, (b + 1) * KC)
                    pe.wait_ge(g_pre, b * 2)
                    for j in range(NTOK):
                        for k in range(KC):
                            ins = nc.tensor.matmul(ab_ps[j // 2][:, j % 2 * D:(j % 2 + 1) * D],
                                                   zT[:, k, j * P:(j + 1) * P], wab[:, k, 0:D],
                                                   start=(k == 0), stop=(k == KC - 1))
                        if j % 2:
                            ins.then_inc(g_ab, 1)
                    pe.wait_ge(g_log, b)
                    for j in range(NTOK):
                        for k in range(KC):
                            ins = nc.tensor.matmul(LG[:, j * NE:(j + 1) * NE], zT[:, k, j * P:(j + 1) * P],
                                                   wab[:, k, D:D + NE], start=(k == 0), stop=(k == KC - 1))
                    ins.then_inc(g_lg, 1)

                def ranks(b, par):
                    pe.wait_ge(g_chosen, b + 1)
                    wait(pe, g_carry, b)
                    wait(pe, g_place, b)
                    v = chosen[:, :, :].rearrange("p j e -> p (j e)")
                    nc.tensor.matmul(PL, before[:, :], v, start=True, stop=False)
                    c = carry[par][:, :].rearrange("p (o e) -> p o e", o=1)
                    nc.tensor.matmul(PL, ones[:, :], c.broadcast_to([P, NTOK, NE]), start=False, stop=False)
                    for j in range(NTOK - 1):
                        n = NTOK - 1 - j
                        src = chosen[:, j:j + 1, :].broadcast_to([P, n, NE])
                        ins = nc.tensor.matmul(PL[:, (j + 1) * NE:NTOK * NE], ones[:, :], src,
                                               start=False, stop=(n == 1))
                    ins.then_inc(g_pl, 1)

                z_now = [None]

                def z_of(b):
                    return z_now[0]

                def step(s, ph, pair):
                    n = PREP + 2 * pair
                    if has(s, 0):
                        z_now[0] = z[ph]
                        gate(s)
                        dense(s)
                    if has(s, -1):
                        ranks(s - 1, (ph + 1) % 2)
                    if has(s, 0):
                        for i in range(NROT):
                            if ph % 2 == 0:
                                product(i, n, gET[:, i], gE[:, i])
                            else:
                                turned(i, n + 1, gE[:, i])

                steps(pe, step)

                pe.wait_ge(g_carry, B)
                pe.wait_ge(g_place, B)
                nc.tensor.matmul(PL[:, 0:NE], ones[:, :], carry[B % 2][:, :], start=True, stop=True).then_inc(g_pl, 1)

                n = PREP + 2 * HALVINGS
                pe.wait_ge(r_v, R_PLUS)
                product(0, n, gET[:, 0], gE[:, 1])
                turned(0, n + 1, prod[:, 0])
                product(0, n + 2, prod[:, 1], gE[:, 2])
                for e in range(NE):
                    i = e % 2
                    if e < 2:
                        pe.wait_ge(r_free[0], n + 3)
                    pe.wait_ge(r_w2[i], 16 * (e // 2 + 1))
                    for half in range(FC // 2):
                        use = ROT_END(i) + (e // 2) * (FC // 2) + half
                        pe.wait_ge(r_free[i], use)
                        for f in range(2):
                            c = (half * 2 + f) * P
                            for k in range(KC):
                                ins = nc.tensor.matmul(rot_ps[i][:, f * D:(f + 1) * D], w2T[i][:, k, c:c + P],
                                                       prod[:, 2, k, :], start=(k == 0), stop=(k == KC - 1))
                        ins.then_inc(r_full[i], 1)
                for k in range(KC):
                    ins = nc.tensor.matmul(rot_ps[2][0:NE, 0:D], eb2T[:, k, :], prod[:, 2, k, :],
                                           start=(k == 0), stop=(k == KC - 1))
                ins.then_inc(r_full[2], 1)

            @block.scalar
            def _(act):
                act.wait_ge(g_load, 4 * 16)

                def copy_rot(i, n, dst):
                    act.wait_ge(r_full[i], n + 1)
                    nc.scalar.copy(dst, rot_ps[i][:, :].rearrange("p (k d) -> p k d", d=D)).then_inc(r_free[i], 1)

                for i in range(NROT):
                    copy_rot(i, len(SERIES), gET[:, i])

                def step(s, ph, pair):
                    if has(s, 0):
                        b = s
                        for k in range(KC):
                            act.wait_ge(g_zt, b * KC + k + 1)
                            if k == 0:
                                act.wait_ge(g_lg, b)
                            nc.scalar.activation(zT[:, k, :], zt_ps[k][:, :], ACT.Identity,
                                                 scale=affine[:, 0, k:k + 1], bias=affine[:, 1, k:k + 1])\
                              .then_inc(g_ztc, 1)
                    if has(s, -1):
                        b = s - 1
                        act.wait_ge(g_pre, (b + 1) * 2)
                        nc.scalar.activation(pre[:, :, :], pre[:, :, :], ACT.Gelu).then_inc(g_abel, 1)
                    if has(s, 0) and ph % 2:
                        for i in range(NROT):
                            copy_rot(i, PREP + 2 * pair + 1, gET[:, i])

                steps(act, step)
                act.wait_ge(g_t, T_DIFF)
                nc.scalar.activation(top[:, :, 1], top[:, :, 1], ACT.Exp).then_inc(g_exp, 1)
                n = PREP + 2 * HALVINGS
                for m in range(3):
                    copy_rot(0, n + m, prod[:, m])
                for e in range(NE):
                    i = e % 2
                    for half in range(FC // 2):
                        copy_rot(i, ROT_END(i) + (e // 2) * (FC // 2) + half, w2[:, e, 2 * half:2 * half + 2, :])
                act.wait_ge(r_full[2], ROT_END(2) + 1)
                nc.scalar.copy(eb2_out[:, :], rot_ps[2][0:NE, 0:D]).then_inc(r_eb, 1)
            @block.vector
            def _(dve):
                nc.vector.memset(ones[:, :], 1.0).then_inc(g_init, 1)
                nc.vector.memset(neg_half[:, :], -0.5).then_inc(g_init, 1)
                nc.vector.memset(neg_halves[:, :, :], -0.5).then_inc(g_init, 1)
                for i in range(2):
                    nc.vector.memset(carry[i][:, :], 0.0).then_inc(g_init, 1)
                nc.vector.memset(zero[:, :, :], 0.0).then_inc(g_init, 1)
                dve.wait_ge(g_load, 4 * 16)
                nc.vector.tensor_copy(before[:, :], cst[:, P:2 * P]).then_inc(g_init, 1)
                dve.wait_ge(r_load, (2 * NROT + 1) * 16)
                nc.vector.tensor_scalar(gA[:, :, :, :], gA[:, :, :, :], 0.5 ** HALVINGS, None, ALU.mult).then_inc(r_v, 1)
                nc.vector.tensor_scalar(gAT[:, :, :, :], gAT[:, :, :, :], 0.5 ** HALVINGS, None, ALU.mult).then_inc(r_v, 1)
                dve.wait_ge(r_v, 2)

                def rot(i):
                    return rot_ps[i][:, :].rearrange("p (k d) -> p k d", d=D)

                for n, c in enumerate(SERIES):
                    for i in range(NROT):
                        dve.wait_ge(r_full[i], n + 1)
                        nc.vector.scalar_tensor_tensor(out=gE[:, i], in0=gA[:, i], scalar=float(c), in1=rot(i),
                                                       op0=ALU.mult, op1=ALU.add).then_inc(r_free[i], 1)
                for i in range(NROT):
                    dve.wait_ge(r_free[i], len(SERIES))
                nc.vector.tensor_scalar(gE[:, :, :, :], gE[:, :, :, :], 1.0 / SERIES[-1], None, ALU.mult).then_inc(r_v, 1)

                def stats(b):
                    for j in range(NTOK):
                        nc.vector.bn_stats(st1[:, j, :], xs[:, b, j, :]).then_inc(g_st, 1)
                    dve.wait_ge(g_st, (b + 1) * NTOK)
                    wait(dve, g_mv1, b)
                    wait(dve, g_z, b * NTOK)
                    plain(dve)
                    for j in range(NTOK):
                        nc.vector.bn_aggr(mv0[:, j, :], st1[:, j, :]).then_inc(g_mv, 1)
                    dve.wait_ge(g_mv, (b + 1) * NTOK)
                    nc.vector.tensor_scalar(ve[:, 0, :], mv0[:, :, 1], EPS, None, ALU.add).then_inc(g_ve, 1)
                    nc.vector.tensor_scalar(ve[:, 1, :], mv0[:, :, 1], 1.0 + EPS, EPS * EPS, ALU.mult, ALU.add)\
                      .then_inc(g_ve, 1)
                    nc.vector.tensor_copy(mv1[:, bass.ds(b * NTOK, NTOK), :], mv0[:, :, :]).then_inc(g_mv1, 1)

                def norm_z(b, ph, fourth):
                    dve.wait_ge(g_rs, b + 1)
                    nc.vector.tensor_copy(rstd1[:, bass.ds(b * NTOK, NTOK)], rs[:, 0, :])
                    wait(dve, g_scat[ph], fourth * NTOK * TOPK * 16)
                    for j in range(NTOK):
                        nc.vector.tensor_scalar(z[ph][:, j, :], xs[:, b, j, :], mv0[:, j, 0:1], rs[:, 1, j:j + 1],
                                                ALU.subtract, ALU.mult).then_inc(g_z, 1)

                def route(b):
                    wait(dve, g_kept, b)
                    wait(dve, g_abst, b * 16)
                    bias = bias_ab[:, 0:D].rearrange("p (o d) -> p o d", o=1).broadcast_to([P, 2, D])
                    for n in range(2):
                        dve.wait_ge(g_ab, b * 2 + n + 1)
                        nc.vector.tensor_tensor(pre[:, 2 * n:2 * n + 2, :],
                                                ab_ps[n][:, :].rearrange("p (j d) -> p j d", d=D), bias, ALU.add)\
                          .then_inc(g_pre, 1)
                    dve.wait_ge(g_lg, b + 1)
                    gbias = bias_ab[:, D:D + NE].rearrange("p (o e) -> p o e", o=1).broadcast_to([P, NTOK, NE])
                    nc.vector.tensor_tensor(logit[:, :, :], LG.rearrange("p (j e) -> p j e", e=NE), gbias, ALU.add)\
                      .then_inc(g_log, 1)
                    dve.wait_ge(g_log, b + 1)
                    plain(dve)
                    for j in range(NTOK):
                        nc.vector.max(best[:, j, :], logit[:, j, :]).then_inc(g_best, 1)
                    dve.wait_ge(g_best, (b + 1) * NTOK)
                    plain(dve)
                    for j in range(NTOK):
                        nc.vector.max_index(best_i[:, j, :], best[:, j, :], logit[:, j, :]).then_inc(g_bi, 1)
                    nc.vector.tensor_copy(top[:, bass.ds(b * NTOK, NTOK), :], best[:, :, 0:TOPK]).then_inc(g_top, 1)
                    dve.wait_ge(g_bi, (b + 1) * NTOK)
                    nc.vector.tensor_copy(best_f[:, :, :], best_i[:, :, 0:TOPK].rearrange("p j s -> p s j"))\
                      .then_inc(g_bf, 1)
                    dve.wait_ge(g_bf, b + 1)
                    iota = numbers.rearrange("p (o e) -> p o e", o=1).broadcast_to([P, NTOK, NE])
                    for s in range(TOPK):
                        mine = best_f[:, s, :].rearrange("p (j o) -> p j o", o=1).broadcast_to([P, NTOK, NE])
                        nc.vector.tensor_tensor(hot[:, s, :, :], iota, mine, ALU.is_equal).then_inc(g_hot, 1)
                    dve.wait_ge(g_hot, (b + 1) * TOPK)
                    dve.wait_ge(g_pl, b)
                    nc.vector.tensor_tensor(chosen[:, :, :], hot[:, 0, :, :], hot[:, 1, :, :], ALU.add)\
                      .then_inc(g_chosen, 1)

                def count(b, par):
                    dve.wait_ge(g_chosen, b + 1)
                    nc.vector.tensor_reduce(batch_sum[:, :], chosen[:, :, :].rearrange("p j e -> p e j"), AX_X, ALU.add)\
                      .then_inc(g_bsum, 1)
                    dve.wait_ge(g_bsum, b + 1)
                    nc.vector.tensor_tensor(carry[1 - par][:, :], carry[par][:, :], batch_sum[:, :], ALU.add)\
                      .then_inc(g_carry, 1)

                def destinations(b, ph):
                    dve.wait_ge(g_pl, b + 1)
                    off = first_row.rearrange("p (o e) -> p o e", o=1).broadcast_to([P, NTOK, NE])
                    nc.vector.tensor_tensor(place[:, :, :], PL.rearrange("p (j e) -> p j e", e=NE), off, ALU.add)\
                      .then_inc(g_place, 1)
                    dve.wait_ge(g_place, b + 1)
                    for s in range(TOPK):
                        nc.vector.tensor_tensor(pick[:, s, :, :], hot[:, s, :, :], place[:, :, :], ALU.mult)\
                          .then_inc(g_pick, 1)
                    dve.wait_ge(g_pick, (b + 1) * TOPK)
                    nc.vector.tensor_reduce(dest_f[:, :, :], pick[:, :, :, :], AX_X, ALU.add).then_inc(g_df, 1)
                    dve.wait_ge(g_df, b + 1)
                    nc.vector.tensor_copy(to_row[ph][:, :, :], dest_f[:, :, :].rearrange("p s j -> p j s"))\
                      .then_inc(g_dest, 1)
                    nc.vector.tensor_copy(region_row[:, bass.ds(b * NTOK, NTOK), :],
                                          dest_f[:, :, :].rearrange("p s j -> p j s")).then_inc(g_kept, 1)

                def square(pair):
                    n = PREP + 2 * pair
                    for i in range(NROT):
                        dve.wait_ge(r_full[i], n + 1)
                        nc.vector.scalar_tensor_tensor(out=gE[:, i], in0=gE[:, i], scalar=2.0, in1=rot(i),
                                                       op0=ALU.mult, op1=ALU.add).then_inc(r_free[i], 1)

                stats(0)
                norm_z(0, 0, 0)
                stats(1)

                def step(s, ph, pair):
                    if has(s, -1):
                        route(s - 1)
                    if has(s, 1):
                        n = s + 1
                        norm_z(n, (ph + 1) % 4, n // 4 if isinstance(n, int) else pair // 2 + (ph == 3))
                    if has(s, -1):
                        count(s - 1, (ph + 1) % 2)
                    if has(s, 2):
                        stats(s + 2)
                    if has(s, 0) and ph % 2:
                        square(pair)
                    if has(s, -1):
                        destinations(s - 1, (ph + 3) % 4)

                steps(dve, step)

                chain = [0]

                def link(ins):
                    chain[0] += 1
                    ins.then_inc(g_t, 1)
                    dve.wait_ge(g_t, chain[0])
                    return chain[0]

                dve.wait_ge(g_top, B)
                dve.wait_ge(g_kept, B)
                at = link(nc.vector.tensor_tensor(top[:, :, 1], top[:, :, 1], top[:, :, 0], ALU.subtract))
                assert at == T_DIFF
                for i in range(NROT):
                    dve.wait_ge(r_free[i], PREP + 2 * HALVINGS)
                for dst in (gE[:, 0], gE[:, 1], gE[:, 2], gET[:, 0]):
                    for k in range(KC):
                        d = dst[:, k, k * P:(k + 1) * P]
                        ins = nc.vector.tensor_tensor(d, d, ident, ALU.add)
                    ins.then_inc(r_v, 1)

                dve.wait_ge(g_exp, 1)
                link(nc.vector.tensor_scalar(top[:, :, 0], top[:, :, 1], 1.0, None, ALU.add))
                link(nc.vector.reciprocal(top[:, :, 0], top[:, :, 0]))
                link(nc.vector.tensor_tensor(top[:, :, 1], top[:, :, 1], top[:, :, 0], ALU.mult))

                dve.wait_ge(g_pl, B + 1)
                count_f, tiles_f, upto = cnt[:, 0, :], cnt[:, 1, :], cnt[:, 2, :]
                link(nc.vector.tensor_copy(count_f, PL[:, 0:NE]))
                link(nc.vector.tensor_tensor(cnt[:, 3, :], count_f, first_row, ALU.add))
                link(nc.vector.tensor_copy(tail[:, :], cnt[:, 3, :]))
                link(nc.vector.tensor_scalar(cnt[:, 4, :], count_f, float(RT - 1), None, ALU.add))
                link(nc.vector.tensor_copy(cnt_i[:, 0, :], cnt[:, 4, :]))
                link(nc.vector.tensor_scalar(cnt_i[:, 1, :], cnt_i[:, 0, :], RT.bit_length() - 1, None,
                                             ALU.arith_shift_right))
                link(nc.vector.tensor_copy(tiles_f, cnt_i[:, 1, :]))
                link(nc.vector.tensor_copy(upto, tiles_f))
                for e in range(1, NE):
                    link(nc.vector.tensor_tensor(upto[:, e:e + 1], upto[:, e - 1:e], tiles_f[:, e:e + 1], ALU.add))
                no, exp_, start, row, live = (tb[:, n, :] for n in range(5))
                link(nc.vector.tensor_scalar(cnt[:, 5, 0:1], upto[:, NE - 1:NE], -1.0, None, ALU.add))
                link(nc.vector.tensor_scalar(no, tile_no, cnt[:, 5, 0:1], None, ALU.min))
                link(nc.vector.tensor_scalar(exp_, no, upto[:, 0:1], None, ALU.is_ge))
                link(nc.vector.tensor_scalar(start, exp_, tiles_f[:, 0:1], None, ALU.mult))
                for e in range(1, NE - 1):
                    link(nc.vector.tensor_scalar(live, no, upto[:, e:e + 1], None, ALU.is_ge))
                    link(nc.vector.tensor_tensor(exp_, exp_, live, ALU.add))
                    link(nc.vector.scalar_tensor_tensor(out=start, in0=live, scalar=tiles_f[:, e:e + 1], in1=start,
                                                        op0=ALU.mult, op1=ALU.add))
                link(nc.vector.tensor_tensor(row, no, start, ALU.subtract))
                link(nc.vector.tensor_scalar(row, row, float(RT), None, ALU.mult))
                link(nc.vector.scalar_tensor_tensor(out=row, in0=exp_, scalar=float(REGION), in1=row,
                                                    op0=ALU.mult, op1=ALU.add))
                link(nc.vector.tensor_copy(table[:, 0, :], exp_))
                link(nc.vector.tensor_copy(table[:, 1, :], row))
                step_e = cnt[:, 3, :]
                link(nc.vector.tensor_scalar(step_e, tiles_f, float(RT), float(-REGION), ALU.mult, ALU.add))
                flat = region_row[:, :, :].rearrange("p t s -> p (t s)")
                moved = shift[:, 0, :]
                link(nc.vector.tensor_copy(moved, flat))
                for e in range(1, NE):
                    link(nc.vector.tensor_scalar(shift[:, 1, :], flat, first_row[:, e:e + 1], step_e[:, e - 1:e],
                                                 ALU.is_ge, ALU.mult))
                    link(nc.vector.tensor_tensor(moved, moved, shift[:, 1, :], ALU.add))
                nc.vector.tensor_copy(result_row[:, :, :].rearrange("p t s -> p (t s)"), moved).then_inc(g_table, 1)

            @block.gpsimd
            def _(pool):
                pool.wait_ge(g_init, 7)

                def inverse(b):
                    pool.wait_ge(g_ve, (b + 1) * 2)
                    nc.gpsimd.tensor_tensor(rs[:, :, :], ve[:, :, :], neg_halves[:, :, :], ALU.pow).then_inc(g_rs, 1)

                inverse(0)
                inverse(1)

                def step(s, ph, pair):
                    if has(s, 2):
                        inverse(s + 2)
                    if has(s, -1):
                        b = s - 1
                        last = (ph + 3) % 4
                        pool.wait_ge(g_dest, b + 1)
                        plain(pool)
                        for j in range(NTOK):
                            for k in range(TOPK):
                                idx = to_row[last][:, j, k:k + 1]
                                pool.indirect_dma_start(z_rows, bass.IndirectOffsetOnAxis(ap=idx, axis=0),
                                                        z[last][:, j, :], None)\
                                    .then_inc(g_scat[last], 16)

                steps(pool, step)
                for i in range(4):
                    pool.wait_ge(g_scat[i], (B // 4) * NTOK * TOPK * 16)

        exp_ctx = ExitStack()
        with exp_ctx:
            def esb(name, shape, dt=F32):
                return sb(name, shape, dt, exp_ctx)

            rows_in = [esb(f"rows_in{i}", [P, RB, D]) for i in range(2)]
            w1c = [esb(f"w1c{i}", [P, KC, F]) for i in range(2)]
            b1c = [esb(f"b1c{i}", [P, FC]) for i in range(2)]
            inT = [esb(f"inT{i}", [P, KC, RT]) for i in range(2)]
            hT = [esb(f"hT{i}", [P, FC, RT]) for i in range(2)]
            rows_out = [esb(f"rows_out{i}", [P, RB, D]) for i in range(2)]

            def ebank(name, n):
                return exp_ctx.enter_context(nc.psum_tensor(name, [P, n], F32))

            in_ps = [ebank(f"in_ps{i}", KC * RT) for i in range(2)]
            h_ps = [ebank(f"h_ps{i}", FC * RT) for i in range(2)]
            o_ps = [ebank(f"o_ps{i}", RB * D) for i in range(2)]

            e_in = [sem(f"e_in{i}") for i in range(2)]
            e_turn_of = [sem(f"e_turn_of{i}") for i in range(2)]
            e_w1 = sem("e_w1")
            e_b1 = sem("e_b1")
            e_inT = sem("e_inT")
            e_h = sem("e_h")
            e_hT = sem("e_hT")
            e_o = sem("e_o")
            e_out = [sem(f"e_out{i}") for i in range(2)]
            e_store = [sem(f"e_store{i}") for i in range(2)]
            block = exp_ctx.enter_context(nc.Block())

            AHEAD = 4

            def tiles(eng, step):
                for t in range(2):
                    step(t, t, 0)
                with eng.Fori(1, (RTILES - AHEAD) // 2) as i:
                    step(2 * i, 0, i)
                    step(2 * i + 1, 1, i)
                for t in range(RTILES - AHEAD, RTILES):
                    step(t, t % 2, t // 2)

            def there(t):
                return not isinstance(t, int) or t < RTILES

            def lookup(eng, which, t, largest):
                return eng.value_load(table[0:1, which, bass.ds(t, 1)], min_val=0, max_val=largest)

            @block.sync
            def _(sp):
                def load(t, par, turn):
                    row = lookup(sp, 1, t, NE * REGION - RT)
                    wait(sp, e_turn_of[par], turn)
                    sp.dma_start(rows_in[par][:, :, :], z_rows[bass.ds(row, RT), :].rearrange("(r p) d -> p r d", p=P))\
                      .then_inc(e_in[par], 16)

                def store(t, par, turn):
                    sp.wait_ge(e_out[par], turn + 1)
                    sp.dma_start(y_rows[bass.ds(t * RT, RT), :].rearrange("(r p) d -> p r d", p=P), rows_out[par][:, :, :])\
                      .then_inc(e_store[par], 16)

                def step(t, par, turn):
                    if there(t + AHEAD):
                        load(t + AHEAD, par, turn + AHEAD // 2)
                    store(t, par, turn)

                for t in range(AHEAD):
                    load(t, t % 2, t // 2)
                tiles(sp, step)
                for i in range(2):
                    sp.wait_ge(e_store[i], 16 * (RTILES // 2))

            @block.scalar
            def _(act):
                def gelu(t, par):
                    act.wait_ge(e_b1, t + 1)
                    wait(act, e_o, t - 1)
                    for f in range(FC):
                        if f % 2 == 0:
                            act.wait_ge(e_h, t * (FC // 2) + f // 2 + 1)
                        nc.scalar.activation(hT[par][:, f, :], h_ps[par][:, f * RT:(f + 1) * RT], ACT.Gelu,
                                             bias=b1c[par][:, f:f + 1]).then_inc(e_hT, 1)

                def step(t, par, turn):
                    if there(t + 1):
                        gelu(t + 1, 1 - par)

                gelu(0, 0)
                tiles(act, step)

            @block.tensor
            def _(pe):
                def turn_rows(t, par, turn):
                    pe.wait_ge(e_in[par], (turn + 1) * 16)
                    wait(pe, e_inT, (t - 1) * KC)
                    for k in range(KC):
                        for r in range(RB):
                            ins = nc.tensor.transpose(in_ps[par][:, k * RT + r * P:k * RT + (r + 1) * P],
                                                      rows_in[par][:, r, k * P:(k + 1) * P], ident)
                    ins.then_inc(e_turn_of[par], 1)

                def hidden(t, par):
                    pe.wait_ge(e_w1, t + 1)
                    pe.wait_ge(e_inT, (t + 1) * KC)
                    wait(pe, e_hT, (t - 1) * FC)
                    for f in range(FC):
                        for k in range(KC):
                            ins = nc.tensor.matmul(h_ps[par][:, f * RT:(f + 1) * RT], w1c[par][:, k, f * P:(f + 1) * P],
                                                   inT[par][:, k, :], start=(k == 0), stop=(k == KC - 1))
                        if f % 2:
                            ins.then_inc(e_h, 1)

                def result(t, par, turn):
                    e = lookup(pe, 0, t, NE - 1)
                    wait(pe, e_out[par], turn)
                    for r in range(RB):
                        for f in range(FC):
                            if r == 0:
                                pe.wait_ge(e_hT, t * FC + f + 1)
                            ins = nc.tensor.matmul(o_ps[par][:, r * D:(r + 1) * D], hT[par][:, f, r * P:(r + 1) * P],
                                                   w2[:, bass.ds(e, 1), f, :].rearrange("p o d -> p (o d)"),
                                                   start=(f == 0), stop=(f == FC - 1))
                    ins.then_inc(e_o, 1)

                def step(t, par, turn):
                    if there(t + 1):
                        hidden(t + 1, 1 - par)
                    if there(t + 2):
                        turn_rows(t + 2, par, turn + 1)
                    result(t, par, turn)

                turn_rows(0, 0, 0)
                hidden(0, 0)
                turn_rows(1, 1, 0)
                tiles(pe, step)

            @block.vector
            def _(dve):
                def weights(t, par):
                    e = lookup(dve, 0, t, NE - 1)
                    wait(dve, e_h, (t - 1) * (FC // 2))
                    nc.vector.tensor_copy(w1c[par][:, :, :], w1[:, bass.ds(e, 1), :, :].rearrange("p o k f -> p (o k) f"))\
                      .then_inc(e_w1, 1)
                    wait(dve, e_hT, (t - 1) * FC)
                    nc.vector.tensor_copy(b1c[par][:, :], b1[:, bass.ds(e, 1), :].rearrange("p o f -> p (o f)"))\
                      .then_inc(e_b1, 1)

                def scale_rows(t, par, turn):
                    dve.wait_ge(e_turn_of[par], turn + 1)
                    for k in range(KC):
                        nc.vector.tensor_scalar(inT[par][:, k, :], in_ps[par][:, k * RT:(k + 1) * RT],
                                                affine[:, 0, k:k + 1], affine[:, 1, k:k + 1], ALU.mult, ALU.add)\
                          .then_inc(e_inT, 1)

                def add_bias(t, par, turn):
                    e = lookup(dve, 0, t, NE - 1)
                    dve.wait_ge(e_o, t + 1)
                    wait(dve, e_store[par], turn * 16)
                    nc.vector.tensor_tensor(rows_out[par][:, :, :], o_ps[par][:, :].rearrange("p (r d) -> p r d", d=D),
                                            b2[:, bass.ds(e, 1), :].broadcast_to([P, RB, D]), ALU.add)\
                      .then_inc(e_out[par], 1)

                def step(t, par, turn):
                    if there(t + 2):
                        weights(t + 2, par)
                        scale_rows(t + 2, par, turn + 1)
                    add_bias(t, par, turn)

                for t in range(2):
                    weights(t, t)
                    scale_rows(t, t, 0)
                tiles(dve, step)

        weights_ctx.close()
        fin_ctx = ExitStack()
        with fin_ctx:
            def fsb(name, shape, dt=F32):
                return sb(name, shape, dt, fin_ctx)

            def two(name, shape, dt=F32):
                return [fsb(f"{name}{i}", shape, dt) for i in range(2)]

            rows = two("rows", [P, TOPK, NTOK, D])
            both = two("both", [P, NTOK, 2, D])
            first = two("first", [P, NTOK, D])
            yn = two("yn", [P, NTOK, D])
            diff = two("diff", [P, NTOK, D])
            base = two("base", [P, NTOK, D])
            u = two("u", [P, NTOK, D])
            o = two("o", [P, NTOK, D])
            gcw = fsb("gcw", [P, 2, D])
            gcb = fsb("gcb", [P, 1])
            junk = fsb("junk", [P, NTOK, 2, D])
            xnorm = fsb("xnorm", [P, TILES, 2])
            share = two("share", [P, NTOK, TOPK])
            xn_b = two("xn_b", [P, NTOK, 2])
            dot = two("dot", [P, NTOK])
            gate = two("gate", [P, NTOK])
            fst = fsb("fst", [P, NTOK, 6])
            fmv = fsb("fmv", [P, NTOK, 2])
            fve = fsb("fve", [P, NTOK])
            frs = two("frs", [P, NTOK])
            fnm = two("fnm", [P, NTOK])
            from_row = two("from_row", [P, NTOK, TOPK], U32)

            f_load = sem("f_load")
            f_idx = sem("f_idx")
            f_rows = [sem(f"f_rows{i}") for i in range(2)]
            f_ab = [sem(f"f_ab{i}") for i in range(2)]
            f_xnorm = sem("f_xnorm")
            f_small = sem("f_small")
            f_first = sem("f_first")
            f_yn = sem("f_yn")
            f_moe = sem("f_moe")
            f_diff = sem("f_diff")
            f_dot = sem("f_dot")
            f_base = sem("f_base")
            f_gate = sem("f_gate")
            f_u = sem("f_u")
            f_st = sem("f_st")
            f_mv = sem("f_mv")
            f_ve = sem("f_ve")
            f_rs = sem("f_rs")
            f_nm = sem("f_nm")
            f_o = sem("f_o")
            f_res = sem("f_res")
            f_out = [sem(f"f_out{i}") for i in range(2)]
            block = fin_ctx.enter_context(nc.Block())

            def steps3(eng, step):
                for s in range(4):
                    step(s, s % 2, s // 2)
                with eng.Fori(2, B // 2 - 1) as i:
                    step(2 * i, 0, i)
                    step(2 * i + 1, 1, i)
                for s in range(B - 2, B + 2):
                    step(s, s % 2, s // 2)

            def doing(s):
                if not isinstance(s, int):
                    return True, True, True
                return s < B, 1 <= s <= B, 2 <= s

            @block.gpsimd
            def _(pool):
                def gather(b, par):
                    nc.gpsimd.tensor_copy(from_row[par][:, :, :], result_row[:, bass.ds(b * NTOK, NTOK), :]).then_inc(f_idx, 1)
                    pool.wait_ge(f_idx, b + 1)
                    plain(pool)
                    for j in range(NTOK):
                        for k in range(TOPK):
                            idx = from_row[par][:, j, k:k + 1]
                            pool.indirect_dma_start(rows[par][:, k, j, :], None, y_rows,
                                                    bass.IndirectOffsetOnAxis(ap=idx, axis=0))\
                                .then_inc(f_rows[par], 16)

                def step(s, par, turn):
                    total, gated, normed = doing(s)
                    if normed:
                        pool.wait_ge(f_ve, s - 1)
                        nc.gpsimd.tensor_tensor(frs[par][:, :], fve[:, :], neg_half[:, :], ALU.pow).then_inc(f_rs, 1)
                    if not isinstance(s, int) or s + 1 < B:
                        wait(pool, f_moe, s * NTOK)
                        gather(s + 1, 1 - par)

                gather(0, 0)
                steps3(pool, step)

            @block.sync
            def _(sp):
                dense = abel_rows.rearrange("(b j p) d -> b p j d", j=NTOK, p=P)
                sp.dma_start(gcw[:, :, :], w["gcw"]).then_inc(f_load, 16)
                sp.dma_start(gcb[:, :], w["gcb"]).then_inc(f_load, 16)

                def store(b, par):
                    sp.wait_ge(f_res, b + 1)
                    for pos, blk, n in RUNS:
                        lo = pos % 2 * BLK
                        sp.dma_start(out[b, blk * BLK:(blk + n) * BLK, :], o[par][lo:lo + n * BLK, pos // 2, :])\
                          .then_inc(f_out[par], 16)

                def step(s, par, turn):
                    total, gated, normed = doing(s)
                    if not isinstance(s, int) or s + 1 < B:
                        wait(sp, f_base, s)
                        sp.dma_start(both[1 - par][:, :, 0, :], dense[s + 1]).then_inc(f_ab[1 - par], 16)
                    if normed:
                        store(s - 2, par)

                sp.dma_start(both[0][:, :, 0, :], dense[0]).then_inc(f_ab[0], 16)
                steps3(sp, step)
                for i in range(2):
                    sp.wait_ge(f_out[i], (B // 2) * len(RUNS) * 16)

            @block.scalar
            def _(act):
                act.wait_ge(f_load, 32)

                def step(s, par, turn):
                    total, gated, normed = doing(s)
                    if gated:
                        b = s - 1
                        act.wait_ge(f_dot, (b + 1) * NTOK)
                        nc.scalar.activation(gate[1 - par][:, :], dot[1 - par][:, :], ACT.Sigmoid, bias=gcb[:, 0:1])\
                          .then_inc(f_gate, 1)
                    if total:
                        b = s
                        act.wait_ge(f_small, (b + 1) * 2)
                        wait(act, f_base, b - 1)
                        plain(act)
                        for j in range(NTOK):
                            nc.scalar.activation(yn[par][:, j, :], xs[:, b, j, :], ACT.Identity,
                                                 scale=xn_b[par][:, j, 0:1], bias=xn_b[par][:, j, 1:2]).then_inc(f_yn, 1)
                        act.wait_ge(f_rows[par], (turn + 1) * NTOK * TOPK * 16)
                        for j in range(NTOK):
                            nc.scalar.activation(first[par][:, j, :], rows[par][:, 0, j, :], ACT.Copy,
                                                 scale=share[par][:, j, 0:1]).then_inc(f_first, 1)
                    if normed:
                        b = s - 2
                        act.wait_ge(f_nm, b + 1)
                        wait(act, f_out[par], (turn - 1) * len(RUNS) * 16)
                        for j in range(NTOK):
                            nc.scalar.activation(o[par][:, j, :], u[par][:, j, :], ACT.Identity,
                                                 scale=frs[par][:, j:j + 1], bias=fnm[par][:, j:j + 1]).then_inc(f_o, 1)

                steps3(act, step)

            @block.vector
            def _(dve):
                nv = nc.vector
                nv.tensor_copy(xnorm[:, :, 0], rstd1[:, :]).then_inc(f_xnorm, 1)
                nv.scalar_tensor_tensor(out=xnorm[:, :, 1], in0=mv1[:, :, 0], scalar=-1.0, in1=rstd1[:, :],
                                        op0=ALU.mult, op1=ALU.mult).then_inc(f_xnorm, 1)
                dve.wait_ge(f_load, 32)
                dve.wait_ge(f_xnorm, 2)

                def small(b, par):
                    nv.tensor_copy(share[par][:, :, :], top[:, bass.ds(b * NTOK, NTOK), :]).then_inc(f_small, 1)
                    nv.tensor_copy(xn_b[par][:, :, :], xnorm[:, bass.ds(b * NTOK, NTOK), :]).then_inc(f_small, 1)

                def total_of(b, par, turn):
                    dve.wait_ge(f_ab[par], (turn + 1) * 16)
                    for j in range(NTOK):
                        dve.wait_ge(f_first, b * NTOK + j + 1)
                        nv.scalar_tensor_tensor(out=both[par][:, j, 1, :], in0=rows[par][:, 1, j, :],
                                                scalar=share[par][:, j, 1:2], in1=first[par][:, j, :],
                                                op0=ALU.mult, op1=ALU.add).then_inc(f_moe, 1)
                    if not isinstance(b, int) or b + 1 < B:
                        small(b + 1, 1 - par)
                    for j in range(NTOK):
                        dve.wait_ge(f_moe, b * NTOK + j + 1)
                        wait(dve, f_gate, b - 1)
                        nv.tensor_tensor_reduce(junk[:, j, :, :], both[par][:, j, :, :], gcw[:, :, :], 1.0, 0.0,
                                                ALU.mult, ALU.add, dot[par][:, j:j + 1]).then_inc(f_dot, 1)
                    nv.tensor_tensor(diff[par][:, :, :], both[par][:, :, 1, :], both[par][:, :, 0, :], ALU.subtract)\
                      .then_inc(f_diff, 1)
                    dve.wait_ge(f_yn, (b + 1) * NTOK)
                    nv.tensor_tensor(base[par][:, :, :], yn[par][:, :, :], both[par][:, :, 0, :], ALU.add)\
                      .then_inc(f_base, 1)

                def gated_of(b, par):
                    dve.wait_ge(f_gate, b + 1)
                    dve.wait_ge(f_diff, b + 1)
                    dve.wait_ge(f_base, b + 1)
                    for j in range(NTOK):
                        nv.scalar_tensor_tensor(out=u[par][:, j, :], in0=diff[par][:, j, :], scalar=gate[par][:, j:j + 1],
                                                in1=base[par][:, j, :], op0=ALU.mult, op1=ALU.add).then_inc(f_u, 1)
                    for j in range(NTOK):
                        dve.wait_ge(f_u, b * NTOK + j + 1)
                        nv.bn_stats(fst[:, j, :], u[par][:, j, :]).then_inc(f_st, 1)
                    dve.wait_ge(f_st, (b + 1) * NTOK)
                    wait(dve, f_nm, b)
                    plain(dve)
                    for j in range(NTOK):
                        nv.bn_aggr(fmv[:, j, :], fst[:, j, :]).then_inc(f_mv, 1)
                    dve.wait_ge(f_mv, (b + 1) * NTOK)
                    nv.tensor_scalar(fve[:, :], fmv[:, :, 1], EPS, None, ALU.add).then_inc(f_ve, 1)

                def step(s, par, turn):
                    total, gated, normed = doing(s)
                    if total:
                        total_of(s, par, turn)
                    if normed:
                        b = s - 2
                        dve.wait_ge(f_rs, b + 1)
                        nv.scalar_tensor_tensor(out=fnm[par][:, :], in0=fmv[:, :, 0], scalar=-1.0, in1=frs[par][:, :],
                                                op0=ALU.mult, op1=ALU.mult).then_inc(f_nm, 1)
                    if gated:
                        gated_of(s - 1, 1 - par)
                    if normed:
                        b = s - 2
                        dve.wait_ge(f_o, (b + 1) * NTOK)
                        nv.tensor_tensor(o[par][:, :, :], o[par][:, :, :], xs[:, b, :, :], ALU.add).then_inc(f_res, 1)

                small(0, 0)
                steps3(dve, step)


def sandwich_kernel(nc, a):
    B, S, D = a["x"].shape
    with ExitStack() as outer:
        xs = outer.enter_context(nc.sbuf_tensor("xs", [P, B, S // P, D], F32))
        attention(nc, outer, a["x"], xs, a["wqkvT"], a["bqk"], a["bv_rep"], a["ident"], a["qrows"], a["krows"])
        ffn(nc, xs, a, a["out"])


def kernel(**inputs):
    import numpy as np
    import concourse.bacc as bacc
    from concourse.bass_utils import run_bass_kernel_spmd

    at = {k[len("L0_attn_"):]: np.asarray(v) for k, v in inputs.items() if k.startswith("L0_attn_")}
    ff = {k[len("L0_ffn_"):]: np.asarray(v) for k, v in inputs.items() if k.startswith("L0_ffn_")}
    x = at["hidden_states"]
    B, S, D = x.shape

    def rep(v):
        return np.broadcast_to(v, (P,) + v.shape)

    def by_feature(v):
        return v.reshape(-1, P).T

    qrows, krows, ident = constants()
    arrays = {
        "x": x,
        "wqkvT": np.concatenate([at["Wq"].T, at["Wk"].T, at["Wv"].T], 1),
        "bqk": np.stack([by_feature(at["bq"]), by_feature(at["bk"])], 2).reshape(P, 2 * D // P),
        "bv_rep": rep(np.stack([at["bv"], at["bv"]])),
        "ident": ident, "qrows": qrows, "krows": krows,
        "consts": ffn_constants(B * S),
        "wab": np.concatenate([ff["abel_w"], ff["moe_gate_w"]], 1),
        "bias_ab": rep(np.concatenate([ff["abel_b"], ff["moe_gate_b"]])),
        "affine": np.stack([by_feature(ff["ln_gamma"]), by_feature(ff["ln_beta"])], 1),
        "gens": ff["gens"], "gensT": ff["gens"].transpose(0, 2, 1),
        "ew1": ff["ew1"], "eb1": ff["eb1"].reshape(NE, -1, P).transpose(2, 0, 1),
        "ew2T": ff["ew2"].transpose(0, 2, 1), "eb2T": ff["eb2"].T,
        "gcw": rep(ff["gc_w"].reshape(2, D)), "gcb": rep(ff["gc_b"]),
    }
    nc = bacc.Bacc("TRN2", target_bir_lowering=False, num_devices=1)
    given, aps = {}, {}
    for name, v in arrays.items():
        v = np.ascontiguousarray(v)
        given[f"in_{name}"] = v
        aps[name] = nc.dram_tensor(f"in_{name}", v.shape, mybir.dt.from_np(v.dtype), kind="ExternalInput").ap()
    aps["out"] = nc.dram_tensor("out_0", x.shape, F32, kind="ExternalOutput").ap()
    sandwich_kernel(nc, aps)
    r = run_bass_kernel_spmd(nc, [given], core_ids=[0])
    return r.results[0]["out_0"]
```
